# Optimizing a Trainium2 kernel written in Bass

```python
import numpy as np
import jax
import jax.numpy as jnp

def _softmax(x, axis=-1):
    return jax.nn.softmax(x, axis=axis)

def _gelu(x):
    return jax.nn.gelu(x, approximate=True)

def _silu(x):
    return jax.nn.silu(x)

def _sigmoid(x):
    return jax.nn.sigmoid(x)

def _layernorm(x, axis=-1, eps=1e-05):
    m = jnp.mean(x, axis=axis, keepdims=True)
    v = jnp.var(x, axis=axis, keepdims=True)
    return (x - m) / jnp.sqrt(v + eps)

def _scatter_add(tgt, idx, src, axis=0):
    return tgt.at[idx].add(src)

def _segment_sum(src, seg, n):
    return jax.ops.segment_sum(src, seg, n)
kernel_name = 'mk_sandwich_d1_jaxref_r8_2dea79'

def setup_inputs(seed: int=0):
    np.random.seed(seed)
    _w = jnp.asarray

    def _L0_attn_setup():
        import jax, jax.numpy as jnp
        import numpy as np
        D = 128
        B, S = (4, 512)
        LR = 0.01
        WD = 0.01
        MAX_ALR = 0.1
        EPS = 1e-08

        def _lmm(params, h):
            for W, b in params:
                h = h + jax.nn.silu(h @ W + b)
            return h

        def _reference_tuple_inner(x, Wk, bk, Wq, bq, Wv, bv, Wlr, blr, W1, b1, W2, b2):
            keys = x @ Wk + bk
            queries = x @ Wq + bq
            values = x @ Wv + bv
            alr = MAX_ALR * jax.nn.sigmoid(x @ Wlr + blr).reshape(-1)
            kf = keys.reshape(-1, D)
            vf = values.reshape(-1, D)
            params = ((W1, b1), (W2, b2))

            def loss_fn(ps):
                pred = _lmm(ps, kf)
                per_tok = jnp.mean((pred - vf) ** 2, axis=-1)
                return jnp.sum(per_tok * alr)
            grads = jax.grad(loss_fn)(params)

            def adamw(p, g):
                return p * (1.0 - LR * WD) - LR * g / (jnp.sqrt(g * g) + EPS)
            new_params = jax.tree_util.tree_map(adamw, params, grads)
            retrieved = _lmm(new_params, queries)
            surprises = jax.tree_util.tree_map(lambda g: -g, grads)
            return (retrieved, *jax.tree_util.tree_leaves(surprises))
        key = jax.random.key(seed)
        ks = jax.random.split(key, 13)
        s = 1.0 / np.sqrt(D)

        def lin(k, shape):
            return jax.random.uniform(k, shape, minval=-s, maxval=s, dtype=jnp.float32)
        return {'x': jax.random.normal(ks[0], (B, S, D), dtype=jnp.float32), 'Wk': lin(ks[1], (D, D)), 'bk': lin(ks[2], (D,)), 'Wq': lin(ks[3], (D, D)), 'bq': lin(ks[4], (D,)), 'Wv': lin(ks[5], (D, D)), 'bv': lin(ks[6], (D,)), 'Wlr': lin(ks[7], (D, 1)), 'blr': lin(ks[8], (1,)), 'W1': lin(ks[9], (D, D)), 'b1': lin(ks[10], (D,)), 'W2': lin(ks[11], (D, D)), 'b2': lin(ks[12], (D,))}
    _L0_attn_in = _L0_attn_setup()

    def _L0_ffn_setup():
        import jax, jax.numpy as jnp
        import numpy as np
        E = 8
        TOP_K = 2
        LN_EPS = 1e-05

        def _layernorm(x, g, b):
            mu = jnp.mean(x, axis=-1, keepdims=True)
            var = jnp.var(x, axis=-1, keepdims=True)
            return (x - mu) * jax.lax.rsqrt(var + LN_EPS) * g + b
        key = jax.random.key(seed)
        ks = jax.random.split(key, 4)
        B, T, H, HF = (4, 256, 128, 256)
        s_in = 1.0 / np.sqrt(H)
        s_hid = 1.0 / np.sqrt(HF)
        return {'x': jax.random.normal(ks[0], (B, T, H), dtype=jnp.float32), 'ln_g': jnp.ones((H,), dtype=jnp.float32), 'ln_b': jnp.zeros((H,), dtype=jnp.float32), 'rW': jax.random.normal(ks[1], (H, E), dtype=jnp.float32) * s_in, 'rb': jnp.zeros((E,), dtype=jnp.float32), 'W1': jax.random.normal(ks[2], (E, H, HF), dtype=jnp.float32) * s_in, 'b1': jnp.zeros((E, HF), dtype=jnp.float32), 'W2': jax.random.normal(ks[3], (E, HF, H), dtype=jnp.float32) * s_hid, 'b2': jnp.zeros((E, H), dtype=jnp.float32)}
    _L0_ffn_in = _L0_ffn_setup()
    _d = {'L0_attn_x': _L0_attn_in['x'], 'L0_attn_Wk': _L0_attn_in['Wk'], 'L0_attn_bk': _L0_attn_in['bk'], 'L0_attn_Wq': _L0_attn_in['Wq'], 'L0_attn_bq': _L0_attn_in['bq'], 'L0_attn_Wv': _L0_attn_in['Wv'], 'L0_attn_bv': _L0_attn_in['bv'], 'L0_attn_Wlr': _L0_attn_in['Wlr'], 'L0_attn_blr': _L0_attn_in['blr'], 'L0_attn_W1': _L0_attn_in['W1'], 'L0_attn_b1': _L0_attn_in['b1'], 'L0_attn_W2': _L0_attn_in['W2'], 'L0_attn_b2': _L0_attn_in['b2'], 'L0_ffn_ln_g': _L0_ffn_in['ln_g'], 'L0_ffn_ln_b': _L0_ffn_in['ln_b'], 'L0_ffn_rW': _L0_ffn_in['rW'], 'L0_ffn_rb': _L0_ffn_in['rb'], 'L0_ffn_W1': _L0_ffn_in['W1'], 'L0_ffn_b1': _L0_ffn_in['b1'], 'L0_ffn_W2': _L0_ffn_in['W2'], 'L0_ffn_b2': _L0_ffn_in['b2']}
    _x0 = _d['L0_attn_x']
    _d['L0_attn_x'] = jax.random.normal(jax.random.fold_in(jax.random.key(seed), 1), (8, 256, 128), dtype=_x0.dtype)
    del _x0
    return _d

def reference(L0_attn_x, L0_attn_Wk, L0_attn_bk, L0_attn_Wq, L0_attn_bq, L0_attn_Wv, L0_attn_bv, L0_attn_Wlr, L0_attn_blr, L0_attn_W1, L0_attn_b1, L0_attn_W2, L0_attn_b2, L0_ffn_ln_g, L0_ffn_ln_b, L0_ffn_rW, L0_ffn_rb, L0_ffn_W1, L0_ffn_b1, L0_ffn_W2, L0_ffn_b2):

    def _L0_attn_ref(x, Wk, bk, Wq, bq, Wv, bv, Wlr, blr, W1, b1, W2, b2):
        import jax, jax.numpy as jnp
        import numpy as np
        D = 128
        B, S = (4, 512)
        LR = 0.01
        WD = 0.01
        MAX_ALR = 0.1
        EPS = 1e-08

        def _lmm(params, h):
            for W, b in params:
                h = h + jax.nn.silu(h @ W + b)
            return h

        def _reference_tuple_inner(x, Wk, bk, Wq, bq, Wv, bv, Wlr, blr, W1, b1, W2, b2):
            keys = x @ Wk + bk
            queries = x @ Wq + bq
            values = x @ Wv + bv
            alr = MAX_ALR * jax.nn.sigmoid(x @ Wlr + blr).reshape(-1)
            kf = keys.reshape(-1, D)
            vf = values.reshape(-1, D)
            params = ((W1, b1), (W2, b2))

            def loss_fn(ps):
                pred = _lmm(ps, kf)
                per_tok = jnp.mean((pred - vf) ** 2, axis=-1)
                return jnp.sum(per_tok * alr)
            grads = jax.grad(loss_fn)(params)

            def adamw(p, g):
                return p * (1.0 - LR * WD) - LR * g / (jnp.sqrt(g * g) + EPS)
            new_params = jax.tree_util.tree_map(adamw, params, grads)
            retrieved = _lmm(new_params, queries)
            surprises = jax.tree_util.tree_map(lambda g: -g, grads)
            return (retrieved, *jax.tree_util.tree_leaves(surprises))
        return _reference_tuple_inner(x, Wk, bk, Wq, bq, Wv, bv, Wlr, blr, W1, b1, W2, b2)[0]

    def _L0_ffn_ref(x, ln_g, ln_b, rW, rb, W1, b1, W2, b2):
        import jax, jax.numpy as jnp
        import numpy as np
        E = 8
        TOP_K = 2
        LN_EPS = 1e-05

        def _layernorm(x, g, b):
            mu = jnp.mean(x, axis=-1, keepdims=True)
            var = jnp.var(x, axis=-1, keepdims=True)
            return (x - mu) * jax.lax.rsqrt(var + LN_EPS) * g + b
        z = _layernorm(x, ln_g, ln_b)
        logits = jnp.einsum('bth,he->bte', z, rW) + rb
        probs = jax.nn.softmax(logits, axis=-1)
        topv, topi = jax.lax.top_k(probs, TOP_K)
        mask = jnp.sum(jax.nn.one_hot(topi, E, dtype=probs.dtype) * topv[..., None], axis=-2)
        denom = jnp.maximum(jnp.sum(mask, axis=-1, keepdims=True), 1e-08)
        w = mask / denom
        hid = jax.nn.gelu(jnp.einsum('bth,ehf->btef', z, W1) + b1, approximate=False)
        outs = jnp.einsum('btef,efh->bteh', hid, W2) + b2
        mixed = jnp.sum(outs * w[..., None], axis=2)
        return x + mixed
    x = L0_attn_x
    x = x + _layernorm(_L0_attn_ref(_layernorm(x, axis=-1), L0_attn_Wk, L0_attn_bk, L0_attn_Wq, L0_attn_bq, L0_attn_Wv, L0_attn_bv, L0_attn_Wlr, L0_attn_blr, L0_attn_W1, L0_attn_b1, L0_attn_W2, L0_attn_b2), axis=-1)
    x = x + _layernorm(_L0_ffn_ref(_layernorm(x, axis=-1), L0_ffn_ln_g, L0_ffn_ln_b, L0_ffn_rW, L0_ffn_rb, L0_ffn_W1, L0_ffn_b1, L0_ffn_W2, L0_ffn_b2), axis=-1)
    return x

_drawn_inputs = setup_inputs


def setup_inputs(seed=0):
    import zlib

    import numpy as np

    out = dict(_drawn_inputs(seed))
    spreads = {'L0_ffn_ln_g': (1.0, 0.2),
     'L0_ffn_ln_b': (0.0, 0.1),
     'L0_ffn_rb': (0.0, 0.1),
     'L0_ffn_b1': (0.0, 0.424),
     'L0_ffn_b2': (0.0, 0.293)}
    factors = {'L0_attn_bv': 2.721}
    for name, (base, spread) in spreads.items():
        noise = np.random.default_rng([zlib.crc32(name.encode()), seed]).standard_normal(out[name].shape)
        drawn = base * np.exp(spread * noise) if base else spread * noise
        out[name] = jnp.asarray(drawn.astype(out[name].dtype))
    for name, factor in factors.items():
        out[name] = (out[name] * factor).astype(out[name].dtype)
    return out
```

```python
from contextlib import ExitStack

import concourse.bass as bass
from concourse import mybir

ALU = mybir.AluOpType
ACT = mybir.ActivationFunctionType
AX_X = mybir.AxisListType.X
F32 = mybir.dt.float32
F32R = mybir.dt.float32r
ENG = mybir.EngineType

P = 128
BLOCK = 512
LN_EPS = 1e-5
LR = 0.01
WD = 0.01
MAX_ALR = 0.1
ADAM_EPS = 1e-8


def memory_and_experts(nc, x, Wk, bk, Wq, bq, Wv, bv, Wlr, blr, W1, b1, W2, b2,
                       ln_g, ln_b, rW, rb, fW1, fb1, fW2, fb2, out):
    B, S, D = x.shape
    E, H, HF = fW1.shape
    N = B * S
    T = N // P
    NB = N // BLOCK
    TB = BLOCK // P
    C = HF // P
    assert D == P and H == P and T == NB * TB
    UNITS = NB * E * C
    UB = E * C
    GRAD_SCALE = 2.0 * MAX_ALR / D

    x_v = x.rearrange("b s d -> (b s) d").rearrange("(p t) d -> p t d", p=P)
    out_v = out.rearrange("b s d -> (b s) d").rearrange("(p t) d -> p t d", p=P)

    with ExitStack() as ctx:
        def sb(name, shape, dt=F32):
            return ctx.enter_context(nc.sbuf_tensor(name, shape, dt))

        def sem(name):
            return ctx.enter_context(nc.semaphore(name))

        bank = [ctx.enter_context(nc.psum_tensor(f"bank{i}", [P, BLOCK], F32)) for i in range(8)]

        x_tok = sb("x_tok", [P, T, D])
        xn_tok = sb("xn_tok", [P, T, D])
        x1_tok = xn_tok
        xnT = sb("xnT", [P, N])
        kT = sb("kT", [P, N])
        vT = sb("vT", [P, N])
        sig1 = sb("sig1", [P, N])
        s1 = sb("s1", [P, N])
        h1T = sb("h1T", [P, N])
        sig2 = sb("sig2", [P, N])
        s2 = sb("s2", [P, N])
        alrT = sb("alrT", [P, N])
        qT = sb("qT", [P, N])
        k_tok = sb("k_tok", [P, T, D])
        h1_tok = sb("h1_tok", [P, T, D])
        dz2_tok = kT[:].rearrange("p (t d) -> p t d", d=D)
        dz1_tok = h1T[:].rearrange("p (t d) -> p t d", d=D)
        hvT, dh1T = vT, vT
        dpT = alrT
        u2T, dz2T = sig2, sig2
        d2T = s2
        u1T, dz1T = sig1, sig1
        d1T = s1
        r_sig1, r_h1T, r_sig2, rT = s1, xnT, s2, vT
        zT = alrT
        u_tok = k_tok
        zt_tok = h1_tok
        w_pad = qT[:].rearrange("p (t d) -> p t d", d=P)
        z_hi = sb("z_hi", [P, N], F32R)
        z_lo = sb("z_lo", [P, N], F32R)
        wT = sb("wT", [P, N], F32R)
        fW_raw = sb("fW_raw", [P, E * HF])
        fW1_hi = sb("fW1_hi", [P, E * HF], F32R)
        fW1_lo = sb("fW1_lo", [P, E * HF], F32R)
        fW2_hi = sb("fW2_hi", [P, E * C * H], F32R)
        fW2_lo = sb("fW2_lo", [P, E * C * H], F32R)
        sel = sb("sel", [P, E, P], F32R)
        RING = 4
        g_buf = [sig1[:, i * BLOCK:(i + 1) * BLOCK] for i in range(RING)]
        t_buf = [s1[:, i * BLOCK:(i + 1) * BLOCK] for i in range(RING)]
        oT = s2
        y_tok = xnT[:].rearrange("p (t d) -> p t d", d=D)
        hi_buf = [sb(f"hi_buf{i}", [P, BLOCK], F32R) for i in range(RING)]
        lo_buf = [sb(f"lo_buf{i}", [P, BLOCK], F32R) for i in range(RING)]

        ident = sb("ident", [P, P])
        NV = 7 + E * C
        rows = sb("rows", [NV, P])
        cols = sb("cols", [P, NV])
        BK, BQ, BV, B1, B2, G, BB, FB1 = range(8)
        wk_sb, wq_sb, wv_sb = (sb(n, [P, P]) for n in ("wk_sb", "wq_sb", "wv_sb"))
        wlr_sb = sb("wlr_sb", [P, 1])
        wlr_b = sb("wlr_b", [P, P])
        blr_b = sb("blr_b", [P, 1])
        w1_sb, w2_sb, w2T_sb = (sb(n, [P, P]) for n in ("w1_sb", "w2_sb", "w2T_sb"))
        w1n, w2n = sb("w1n", [P, P]), sb("w2n", [P, P])
        adam_tmp = sb("adam_tmp", [P, 2, P])
        gb = sb("gb", [P, 2, NB])
        gbs = sb("gbs", [P, 2])
        gb_tmp = sb("gb_tmp", [P, 2])
        bn = sb("bn", [P, 2])
        rw_sb = sb("rw_sb", [P, E])
        rb_b = sb("rb_b", [P, E])
        b2_stack = sb("b2_stack", [P, H])
        b2_hi = sb("b2_hi", [P, H], F32R)
        b2_lo = sb("b2_lo", [P, H], F32R)
        stats = sb("stats", [P, T, 6])
        LX, LR_, L1, LZ, LY = range(5)
        mv = sb("mv", [P, 5, T, 2])
        vpe = sb("vpe", [P, 5, T])
        rstd = sb("rstd", [P, 5, T])
        nmean = sb("nmean", [P, 5, T])
        r2 = sb("r2", [P, 2, T])
        minus_half = sb("minus_half", [P, TB])
        ramp = sb("ramp", [P, T, E])
        lg, ex, pr, eq, oh1, oh2 = (kT[:, i * T * E:(i + 1) * T * E].rearrange("p (t e) -> p t e", e=E)
                                    for i in range(6))
        w_hi = sb("w_hi", [P, T, E], F32R)
        red = kT[:, 6 * T * E:7 * T * E].rearrange("p (i t) -> p i t", t=T)

        x_in = [sem(f"x_in{i}") for i in range(NB)]
        rows_in, wk_in, wq_in, wv_in, wlr_in, blr_in = (sem(n) for n in (
            "rows_in", "wk_in", "wq_in", "wv_in", "wlr_in", "blr_in"))
        w1_in, w2_in, rw_in, rb_in, fw1_in, fw2_in, b2s_in = (sem(n) for n in (
            "w1_in", "w2_in", "rw_in", "rb_in", "fw1_in", "fw2_in", "b2s_in"))
        out_done = sem("out_done")
        zeroed, ident_ready, half_ready, ramp_ready, wpad_zero, b2_zero = (sem(n) for n in (
            "zeroed", "ident_ready", "half_ready", "ramp_ready", "wpad_zero", "b2_zero"))
        wlrb_ready, sel_ready, fw_hi_done, fw_lo_done, b2hi_done, b2lo_done = (sem(n) for n in (
            "wlrb_ready", "sel_ready", "fw_hi_done", "fw_lo_done", "b2hi_done", "b2lo_done"))
        dve_step = sem("dve_step")
        vpe_ready = [sem(f"vpe_ready{i}") for i in range(5)]
        rstd_ready = [sem(f"rstd_ready{i}") for i in range(5)]
        xn_ready, vecs_tr, cols_ready, w2T_tr, w2T_ready = (sem(n) for n in (
            "xn_ready", "vecs_tr", "cols_ready", "w2T_tr", "w2T_ready"))
        xn_tr, xnT_ready, k_mm, kT_ready, v_mm, vT_ready, z1_mm, sig1_ready = (sem(n) for n in (
            "xn_tr", "xnT_ready", "k_mm", "kT_ready", "v_mm", "vT_ready", "z1_mm", "sig1_ready"))
        s1_done, h1_done, hv_done, alr_mm, alr_ready, z2_mm, sig2_ready, s2_done = (sem(n) for n in (
            "s1_done", "h1_done", "hv_done", "alr_mm", "alr_ready", "z2_mm", "sig2_ready", "s2_done"))
        e_done, u2_done, d2_done, dz2_done, dh1_mm, dh1_done, u1_done, d1_done, dz1_done = (
            sem(n) for n in ("e_done", "u2_done", "d2_done", "dz2_done", "dh1_mm", "dh1_done",
                             "u1_done", "d1_done", "dz1_done"))
        tok_tr, tok_out, q_mm, qT_ready, gw2_mm, gw1_mm, w2n_ready, w1n_ready, bn_ready = (
            sem(n) for n in ("tok_tr", "tok_out", "q_mm", "qT_ready", "gw2_mm", "gw1_mm",
                             "w2n_ready", "w1n_ready", "bn_ready"))
        rz1_mm, rsig1_ready, rh1_done, rz2_mm, rsig2_ready, r_done, r_tr = (sem(n) for n in (
            "rz1_mm", "rsig1_ready", "rh1_done", "rz2_mm", "rsig2_ready", "r_done", "r_tr"))
        nb_ready, rn_ready, x1_ready, zt_ready, u_ready, zt_tr, zT_ready, zhi_done, zlo_done = (
            sem(n) for n in ("nb_ready", "rn_ready", "x1_ready", "zt_ready", "u_ready", "zt_tr",
                             "zT_ready", "zhi_done", "zlo_done"))
        lg_mm, lg_shift, ex_ready, w_ready, w_tr, wT_ready = (sem(n) for n in (
            "lg_mm", "lg_shift", "ex_ready", "w_ready", "w_tr", "wT_ready"))
        rs1_done, rs2_done, nmr_ready, nm1_ready, lg_read, dp_done = (sem(n) for n in (
            "rs1_done", "rs2_done", "nmr_ready", "nm1_ready", "lg_read", "dp_done"))
        h_mm, g_done, wb_mm, t_done, hi_done, lo_done, y_mm = (sem(n) for n in (
            "h_mm", "g_done", "wb_mm", "t_done", "hi_done", "lo_done", "y_mm"))
        acc_mm, oT_ready, o_tr, y_ready, yn_done = (sem(n) for n in (
            "acc_mm", "oT_ready", "o_tr", "y_ready", "yn_done"))

        SKEW = {"norm_r": 0, "center_r": 1, "norm_x1": 2, "norm_z": 3, "scale_z": 4}
        SCHEDULE = [(what, i - lag) for i in range(NB + 4) for what, lag in SKEW.items() if 0 <= i - lag < NB]

        H_AHEAD, T_AHEAD, HI_AHEAD, LO_AHEAD = 3, 2, 2, 1
        EPILOGUE = {2: 0, 6: 1, 10: 2}

        def ahead(step, j, i, last):
            if i < UB:
                step(j, i)
            elif not last:
                step(j + 1, i - UB)

        def tiles(b):
            return range(TB * b, TB * b + TB)

        def cut(tensor, b):
            return tensor[:, b * BLOCK:(b + 1) * BLOCK]

        def tok(tensor, b):
            return tensor[:, TB * b:TB * b + TB, :]

        def col(i):
            return cols[:, i:i + 1]

        def bank3(i):
            return bank[i][:].rearrange("p (t d) -> p t d", d=P)

        block = ctx.enter_context(nc.Block())

        @block.sync
        def _(sp):
            for b in range(NB):
                sp.dma_start(tok(x_tok, b), tok(x_v, b)).then_inc(x_in[b], 16)
            sp.dma_start(wk_sb[:], Wk).then_inc(wk_in, 16)
            sp.dma_start(wv_sb[:], Wv).then_inc(wv_in, 16)
            sp.dma_start(w1_sb[:], W1).then_inc(w1_in, 16)
            sp.dma_start(w2_sb[:], W2).then_inc(w2_in, 16)
            sp.dma_start(wq_sb[:], Wq).then_inc(wq_in, 16)
            sp.dma_start(fW_raw[:].rearrange("p (e f) -> p e f", f=HF),
                         fW1.rearrange("e h f -> h e f")).then_inc(fw1_in, 16)
            sp.wait_ge(fw_lo_done, 1)
            sp.dma_start(fW_raw[:].rearrange("p (e h) -> p e h", h=H),
                         fW2.rearrange("e (c f) h -> f (e c) h", f=P)).then_inc(fw2_in, 16)
            for b in range(NB):
                sp.wait_ge(yn_done, b + 1)
                sp.dma_start(tok(out_v, b), tok(x1_tok, b)).then_inc(out_done, 16)
            sp.wait_ge(out_done, 16 * NB)

        @block.gpsimd
        def _(pool):
            pool.memset(ident[:], 0.0).then_inc(zeroed, 1)
            pool.wait_ge(zeroed, 1)
            pool.affine_select(out=ident[:], in_=ident[:], compare_op=ALU.not_equal, fill=1.0, base=0,
                               pattern=[[-1, P]], channel_multiplier=1).then_inc(ident_ready, 1)
            pool.memset(minus_half[:], -0.5).then_inc(half_ready, 1)
            pool.wait_ge(half_ready, 1)

            def rsqrt(ln, b):
                pool.wait_ge(vpe_ready[ln], b + 1)
                pool.tensor_tensor(rstd[:, ln, TB * b:TB * b + TB], vpe[:, ln, TB * b:TB * b + TB],
                                   minus_half[:], ALU.pow).then_inc(rstd_ready[ln], 1)

            rsqrt(LX, 0)
            rsqrt(LX, 1)
            pool.wait_ge(wlr_in, 16)
            pool.tensor_scalar(wlr_b[:], wlr_sb[:].to_broadcast([P, P]), 1.0, 0.0, ALU.mult,
                               ALU.add).then_inc(wlrb_ready, 1)
            rsqrt(LX, 2)
            rsqrt(LX, 3)
            pool.iota(ramp[:], pattern=[[0, T], [-1, E]], base=E, channel_multiplier=0,
                      allow_small_or_imprecise_dtypes=True).then_inc(ramp_ready, 1)

            def split_weights(n, loaded, hi, lo):
                pool.wait_ge(loaded, 16)
                pool.tensor_scalar(hi[:], fW_raw[:], 1.0, 0.0, ALU.mult, ALU.add).then_inc(fw_hi_done, 1)
                pool.wait_ge(fw_hi_done, n)
                pool.tensor_tensor(lo[:], fW_raw[:], hi[:].bitcast(F32), ALU.subtract).then_inc(fw_lo_done, 1)

            split_weights(1, fw1_in, fW1_hi, fW1_lo)
            for b in range(NB):
                pool.wait_ge(h1_done, b + 1)
                pool.wait_ge(vT_ready, b + 1)
                pool.tensor_tensor(cut(hvT, b), cut(h1T, b), cut(vT, b), ALU.subtract).then_inc(hv_done, 1)
            for b in range(NB):
                pool.wait_ge(u2_done, b + 1)
                pool.tensor_tensor(cut(d2T, b), cut(s2, b), cut(u2T, b), ALU.subtract).then_inc(d2_done, 1)
                pool.wait_ge(u1_done, b + 1)
                pool.tensor_tensor(cut(d1T, b), cut(s1, b), cut(u1T, b), ALU.subtract).then_inc(d1_done, 1)
            split_weights(2, fw2_in, fW2_hi, fW2_lo)
            pool.wait_ge(ident_ready, 1)
            pool.tensor_tensor(sel[:], ident[:, 0:E].unsqueeze(2).to_broadcast([P, E, P]),
                               ident[:, E:2 * E].unsqueeze(2).to_broadcast([P, E, P]),
                               ALU.add).then_inc(sel_ready, 1)
            pool.wait_ge(b2s_in, 32)
            pool.tensor_scalar(b2_hi[:], b2_stack[:], 1.0, 0.0, ALU.mult, ALU.add).then_inc(b2hi_done, 1)
            pool.wait_ge(b2hi_done, 1)
            pool.tensor_tensor(b2_lo[:], b2_stack[:], b2_hi[:].bitcast(F32),
                               ALU.subtract).then_inc(b2lo_done, 1)
            pool.wait_ge(rh1_done, NB)
            pool.memset(w_pad, 0.0).then_inc(wpad_zero, 1)
            for what, b in SCHEDULE:
                if what == "norm_r":
                    rsqrt(LR_, b)
                if what == "norm_x1":
                    rsqrt(L1, b)
                if what == "norm_z":
                    rsqrt(LZ, b)
                if what == "scale_z":
                    pool.wait_ge(zT_ready, b + 1)
                    pool.tensor_scalar(cut(z_hi, b), cut(zT, b), 1.0, 0.0, ALU.mult,
                                       ALU.add).then_inc(zhi_done, 1)
            for b in range(NB):
                pool.wait_ge(nm1_ready, b + 1)
                for t in tiles(b):
                    last = pool.tensor_scalar(u_tok[:, t, :], x1_tok[:, t, :], rstd[:, L1, t:t + 1],
                                              nmean[:, L1, t:t + 1], ALU.mult, ALU.add)
                last.then_inc(u_ready, 1)

            for b in range(NB):
                rsqrt(LY, b)

        @block.tensor
        def _(pe):
            def mm(out_, lhsT, rhs, start=True, stop=True):
                return pe.matmul(out_, lhsT, rhs, start=start, stop=stop)

            pe.wait_ge(ident_ready, 1)
            pe.wait_ge(rows_in, 16 * 8)
            pe.transpose(bank[7][:, 0:NV], rows[:, :], ident[0:NV, 0:NV]).then_inc(vecs_tr, 1)
            pe.wait_ge(w2_in, 16)
            pe.transpose(bank[7][:, P:2 * P], w2_sb[:], ident[:]).then_inc(w2T_tr, 1)

            def xn_transpose(b):
                pe.wait_ge(xn_ready, b + 1)
                if b >= 2:
                    pe.wait_ge(xnT_ready, b - 1)
                for i, t in enumerate(tiles(b)):
                    last = pe.transpose(bank[b % 2][:, i * P:(i + 1) * P], xn_tok[:, t, :], ident[:])
                last.then_inc(xn_tr, 1)

            def k_product(b):
                pe.wait_ge(wk_in, 16)
                pe.wait_ge(xnT_ready, b + 1)
                if b:
                    pe.wait_ge(kT_ready, b)
                mm(bank[2][:], wk_sb[:], cut(xnT, b)).then_inc(k_mm, 1)

            def v_product(b):
                pe.wait_ge(wv_in, 16)
                if b:
                    pe.wait_ge(vT_ready, b)
                mm(bank[3][:], wv_sb[:], cut(xnT, b)).then_inc(v_mm, 1)

            def z1_product(b):
                pe.wait_ge(w1_in, 16)
                pe.wait_ge(kT_ready, b + 1)
                if b >= 2:
                    pe.wait_ge(sig1_ready, b - 1)
                    pe.wait_ge(s1_done, b - 1)
                mm(bank[4 + b % 2][:], w1_sb[:], cut(kT, b)).then_inc(z1_mm, 1)

            def alr_product(b):
                pe.wait_ge(wlrb_ready, 1)
                if b == 1:
                    pe.wait_ge(cols_ready, 1)
                    pe.wait_ge(w2T_ready, 1)
                if b >= 2:
                    pe.wait_ge(alr_ready, b - 1)
                mm(bank[6 + b % 2][:], wlr_b[:], cut(xnT, b)).then_inc(alr_mm, 1)

            def z2_product(b):
                pe.wait_ge(h1_done, b + 1)
                if b < 2:
                    pe.wait_ge(xnT_ready, b + 3)
                else:
                    pe.wait_ge(sig2_ready, b - 1)
                    pe.wait_ge(s2_done, b - 1)
                mm(bank[b % 2][:], w2_sb[:], cut(h1T, b)).then_inc(z2_mm, 1)

            def token_major(n, source, b, ready, count):
                pe.wait_ge(ready, count)
                if n == 0:
                    pe.wait_ge(kT_ready, NB)
                elif n == 1:
                    pe.wait_ge(vT_ready, NB)
                else:
                    pe.wait_ge(tok_out, n - 1)
                for i in range(TB):
                    last = pe.transpose(bank[2 + n % 2][:, i * P:(i + 1) * P],
                                        source[:, b * BLOCK + i * P:b * BLOCK + (i + 1) * P], ident[:])
                last.then_inc(tok_tr, 1)

            def q_product(b):
                pe.wait_ge(wq_in, 16)
                if b:
                    pe.wait_ge(qT_ready, b)
                mm(bank[4][:], wq_sb[:], cut(xnT, b)).then_inc(q_mm, 1)

            def dh1_product(b):
                pe.wait_ge(w2T_ready, 1)
                pe.wait_ge(dz2_done, b + 1)
                if b < 2:
                    pe.wait_ge(alr_ready, b + 3)
                else:
                    pe.wait_ge(dh1_done, b - 1)
                mm(bank[6 + b % 2][:], w2T_sb[:], cut(dz2T, b)).then_inc(dh1_mm, 1)

            def gradient(into, left, right, b, out_count, done):
                pe.wait_ge(tok_out, out_count)
                for t in tiles(b):
                    last = mm(into, left[:, t, :], right[:, t, :], start=(t == 0), stop=(t == T - 1))
                if b == NB - 1:
                    last.then_inc(done, 1)

            xn_transpose(0)
            k_product(0)
            xn_transpose(1)
            v_product(0)
            for b in range(1, NB):
                z1_product(b - 1)
                k_product(b)
                if b + 1 < NB:
                    xn_transpose(b + 1)
                v_product(b)
            z1_product(NB - 1)
            for b in range(NB):
                alr_product(b)
                z2_product(b)
            for b in range(NB):
                token_major(2 * b, kT, b, kT_ready, b + 1)
                token_major(2 * b + 1, h1T, b, h1_done, b + 1)
            pe.wait_ge(sig1_ready, NB)
            pe.wait_ge(s1_done, NB)
            q_product(0)
            for b in range(NB):
                dh1_product(b)
                token_major(2 * NB + b, dz2T, b, dz2_done, b + 1)
                if b + 1 < NB:
                    q_product(b + 1)
                gradient(bank[5][:, 0:P], h1_tok, dz2_tok, b, 2 * NB + b + 1, gw2_mm)
            pe.wait_ge(s2_done, NB)
            for b in range(NB):
                token_major(3 * NB + b, dz1T, b, dz1_done, b + 1)
            for b in range(NB):
                gradient(bank[1][:, 0:P], k_tok, dz1_tok, b, 3 * NB + b + 1, gw1_mm)

            for b in range(NB):
                if b == 0:
                    pe.wait_ge(w1n_ready, 1)
                    pe.wait_ge(qT_ready, NB)
                if b >= 2:
                    pe.wait_ge(rsig1_ready, b - 1)
                    pe.wait_ge(rs1_done, b - 1)
                mm(bank[4 + b % 2][:], w1n[:], cut(qT, b)).then_inc(rz1_mm, 1)
            for b in range(NB):
                pe.wait_ge(rh1_done, b + 1)
                if b == 0:
                    pe.wait_ge(w2n_ready, 1)
                if b < 2:
                    pe.wait_ge(dh1_done, b + 3)
                else:
                    pe.wait_ge(rsig2_ready, b - 1)
                    pe.wait_ge(rs2_done, b - 1)
                mm(bank[6 + b % 2][:], w2n[:], cut(r_h1T, b)).then_inc(rz2_mm, 1)

            def r_transpose(b):
                pe.wait_ge(r_done, b + 1)
                if b < 2:
                    pe.wait_ge(tok_out, 4 * NB)
                else:
                    pe.wait_ge(rn_ready, b - 1)
                for i in range(TB):
                    last = pe.transpose(bank[2 + b % 2][:, i * P:(i + 1) * P],
                                        rT[:, b * BLOCK + i * P:b * BLOCK + (i + 1) * P], ident[:])
                last.then_inc(r_tr, 1)

            def z_transpose(b):
                pe.wait_ge(zt_ready, b + 1)
                if b >= 2:
                    pe.wait_ge(zT_ready, b - 1)
                for i, t in enumerate(tiles(b)):
                    last = pe.transpose(bank[b % 2][:, i * P:(i + 1) * P], zt_tok[:, t, :], ident[:])
                last.then_inc(zt_tr, 1)

            def logits(b):
                pe.wait_ge(zT_ready, b + 1)
                if b == 0:
                    pe.wait_ge(rw_in, 16)
                    pe.wait_ge(rs1_done, NB - 1)
                for t in tiles(b):
                    last = mm(bank[4][:, t * E:(t + 1) * E], zT[:, t * P:(t + 1) * P], rw_sb[:])
                last.then_inc(lg_mm, 1)

            for b in range(NB):
                r_transpose(b)
            for b in range(NB):
                z_transpose(b)
                logits(b)

            def w_transpose(b):
                if b == 0:
                    pe.wait_ge(w_ready, 1)
                    pe.wait_ge(lg_read, 1)
                if b >= 2:
                    pe.wait_ge(wT_ready, b - 1)
                for i, t in enumerate(tiles(b)):
                    last = pe.transpose(bank[4 + b % 2][:, i * P:(i + 1) * P], w_pad[:, t, :], ident[:])
                last.then_inc(w_tr, 1)

            for b in range(NB):
                w_transpose(b)

            def product3(into, w_hi, w_lo, a_hi, a_lo, start, stop):
                mm(into, w_hi, a_hi, start=start, stop=False)
                mm(into, w_lo, a_hi, start=False, stop=False)
                return mm(into, w_hi, a_lo, start=False, stop=stop)

            def hidden(j, i):
                e, c = divmod(i, C)
                s = slice(e * HF + c * P, e * HF + (c + 1) * P)
                if c == 0:
                    if not (type(j) is int and j == 0 and i < 2 * C):
                        pe.wait_ge(t_done, j * UB + (i - C))
                    mm(bank[2 + e % 2][:], sel[:, e, :], wT[:, bass.ts(j, BLOCK)]).then_inc(wb_mm, 1)
                if not (type(j) is int and j == 0 and i < 2):
                    pe.wait_ge(g_done, j * UB + (i - 1))
                product3(bank[i % 2][:], fW1_hi[:, s], fW1_lo[:, s], z_hi[:, bass.ts(j, BLOCK)],
                         z_lo[:, bass.ts(j, BLOCK)], True, True).then_inc(h_mm, 1)

            def output(j, i):
                s = slice(i * H, (i + 1) * H)
                pe.wait_ge(lo_done, j * UB + (i + 1))
                product3(bank[6][:], fW2_hi[:, s], fW2_lo[:, s], hi_buf[i % RING][:], lo_buf[i % RING][:],
                         False, i == UB - 1).then_inc(y_mm, 1)

            def bias_term(j):
                pe.wait_ge(oT_ready, j + 1)
                mm(bank[6][:], b2_hi[:], wT[:, bass.ts(j, BLOCK)], start=True, stop=False)
                mm(bank[6][:], b2_lo[:], wT[:, bass.ts(j, BLOCK)], start=False, stop=False)

            def final_transpose(b):
                pe.wait_ge(oT_ready, b + 2)
                if b:
                    pe.wait_ge(y_ready, b)
                for i in range(TB):
                    last = pe.transpose(bank[5][:, i * P:(i + 1) * P],
                                        oT[:, b * BLOCK + i * P:b * BLOCK + (i + 1) * P], ident[:])
                last.then_inc(o_tr, 1)

            pe.sem_inc(y_mm, RING)
            pe.wait_ge(sel_ready, 1)
            pe.wait_ge(fw_hi_done, 2)
            pe.wait_ge(fw_lo_done, 2)
            pe.wait_ge(b2lo_done, 1)
            pe.wait_ge(zhi_done, NB)
            pe.wait_ge(zlo_done, NB)
            pe.wait_ge(wT_ready, NB)
            for i in range(H_AHEAD):
                hidden(0, i)

            def body(j, last):
                for i in range(UB):
                    ahead(hidden, j, i + H_AHEAD, last)
                    if i == 0:
                        bias_term(j)
                    output(j, i)
                    if last and i in EPILOGUE:
                        final_transpose(EPILOGUE[i])
                pe.wait_ge(y_mm, j * UB + (UB + RING))
                pe.sem_inc(acc_mm, 1)

            with pe.Fori(0, NB - 1) as j:
                body(j, False)
            body(NB - 1, True)
            final_transpose(NB - 1)

        @block.scalar
        def _(act):
            def dma(dst, src, s):
                act.dma_start(dst, src).then_inc(s, 16)

            def row(v):
                return v.rearrange("(a d) -> a d", a=1)

            for i, v in enumerate((bk, bq, bv, b1, b2, ln_g, ln_b)):
                dma(rows[i:i + 1, :], row(v), rows_in)
            dma(rows[7:NV, :], fb1.rearrange("e (c f) -> (e c) f", f=P), rows_in)
            dma(wlr_sb[:], Wlr, wlr_in)
            dma(blr_b[:], row(blr).to_broadcast([P, 1]), blr_in)
            dma(rw_sb[:], rW, rw_in)
            dma(rb_b[:], row(rb).to_broadcast([P, E]), rb_in)
            act.wait_ge(b2_zero, 1)
            for i in range(2):
                dma(b2_stack[i * E:(i + 1) * E, :], fb2, b2s_in)

            def copy(dst, src, s, **kw):
                act.activation(dst, src, ACT.Identity, **kw).then_inc(s, 1)

            act.wait_ge(vecs_tr, 1)
            act.wait_ge(w2T_tr, 1)
            copy(cols[:], bank[7][:, 0:NV], cols_ready)
            act.wait_ge(cols_ready, 1)
            copy(w2T_sb[:], bank[7][:, P:2 * P], w2T_ready)

            def xnT_out(b):
                act.wait_ge(xn_tr, b + 1)
                copy(cut(xnT, b), bank[b % 2][:], xnT_ready)

            def kT_out(b):
                act.wait_ge(k_mm, b + 1)
                copy(cut(kT, b), bank[2][:], kT_ready, bias=col(BK))

            def vT_out(b):
                act.wait_ge(v_mm, b + 1)
                copy(cut(vT, b), bank[3][:], vT_ready, bias=col(BV))

            def sigmoid(b, product, count, source, into, bias, s):
                act.wait_ge(product, count)
                act.activation(cut(into, b), source[:], ACT.Sigmoid, bias=bias).then_inc(s, 1)

            def sig1_out(b):
                sigmoid(b, z1_mm, b + 1, bank[4 + b % 2], sig1, col(B1), sig1_ready)

            xnT_out(0)
            kT_out(0)
            xnT_out(1)
            vT_out(0)
            for b in range(1, NB):
                sig1_out(b - 1)
                kT_out(b)
                if b + 1 < NB:
                    xnT_out(b + 1)
                vT_out(b)
            sig1_out(NB - 1)
            act.wait_ge(blr_in, 16)
            for b in range(NB):
                sigmoid(b, alr_mm, b + 1, bank[6 + b % 2], alrT, blr_b[:], alr_ready)
                sigmoid(b, z2_mm, b + 1, bank[b % 2], sig2, col(B2), sig2_ready)

            def token_major_out(n, into, b):
                act.wait_ge(tok_tr, n + 1)
                act.activation(tok(into, b), bank3(2 + n % 2), ACT.Identity).then_inc(tok_out, 1)

            def qT_out(b):
                act.wait_ge(q_mm, b + 1)
                copy(cut(qT, b), bank[4][:], qT_ready, bias=col(BQ))

            for b in range(NB):
                token_major_out(2 * b, k_tok, b)
                token_major_out(2 * b + 1, h1_tok, b)
            qT_out(0)
            for b in range(NB):
                token_major_out(2 * NB + b, dz2_tok, b)
                if b + 1 < NB:
                    qT_out(b + 1)
            for b in range(NB):
                token_major_out(3 * NB + b, dz1_tok, b)

            act.wait_ge(bn_ready, 1)
            for b in range(NB):
                if b == 0:
                    act.wait_ge(dz1_done, NB)
                sigmoid(b, rz1_mm, b + 1, bank[4 + b % 2], r_sig1, bn[:, 0:1], rsig1_ready)
            for b in range(NB):
                sigmoid(b, rz2_mm, b + 1, bank[6 + b % 2], r_sig2, bn[:, 1:2], rsig2_ready)

            def center_r(b):
                act.wait_ge(nmr_ready, b + 1)
                for i, t in enumerate(tiles(b)):
                    last = act.activation(x1_tok[:, t, :], bank[2 + b % 2][:, i * P:(i + 1) * P], ACT.Identity,
                                          scale=rstd[:, LR_, t:t + 1], bias=nmean[:, LR_, t:t + 1])
                last.then_inc(rn_ready, 1)

            def zT_out(b):
                act.wait_ge(zt_tr, b + 1)
                copy(cut(zT, b), bank[b % 2][:], zT_ready, scale=col(G), bias=col(BB))

            for what, b in SCHEDULE:
                if what == "center_r":
                    center_r(b)
                if what == "scale_z":
                    zT_out(b)
            act.wait_ge(lg_shift, 1)
            act.activation(ex, lg, ACT.Exp).then_inc(ex_ready, 1)
            for b in range(NB):
                act.wait_ge(w_tr, b + 1)
                copy(cut(wT, b), bank[4 + b % 2][:], wT_ready)

            def gelu(j, i):
                act.wait_ge(h_mm, j * UB + (i + 1))
                if not (type(j) is int and j == 0 and i < H_AHEAD):
                    act.wait_ge(t_done, j * UB + (i - (RING - 2)))
                act.activation(g_buf[i % RING], bank[i % 2][:], ACT.Gelu,
                               bias=col(FB1 + i)).then_inc(g_done, 1)

            def hi(j, i):
                act.wait_ge(t_done, j * UB + (i + 1))
                act.wait_ge(y_mm, j * UB + (i + 1))
                copy(hi_buf[i % RING][:], t_buf[i % RING], hi_done)

            act.sem_inc(oT_ready, 1)
            for i in range(H_AHEAD):
                gelu(0, i)
                if i < HI_AHEAD:
                    hi(0, i)

            def body(j, last):
                for i in range(UB):
                    ahead(gelu, j, i + H_AHEAD, last)
                    ahead(hi, j, i + HI_AHEAD, last)
                act.wait_ge(acc_mm, j + 1)
                act.activation(oT[:, bass.ts(j, BLOCK)], bank[6][:], ACT.Identity).then_inc(oT_ready, 1)

            with act.Fori(0, NB - 1) as j:
                body(j, False)
            body(NB - 1, True)

        @block.vector
        def _(dve):
            steps = [0]

            def link(ins):
                steps[0] += 1
                ins.then_inc(dve_step, 1)
                dve.wait_ge(dve_step, steps[0])

            def span(b):
                return slice(TB * b, TB * b + TB)

            def statistics(ln, b, source):
                for i, t in enumerate(tiles(b)):
                    last = dve.bn_stats(stats[:, t, :], source(i, t))
                link(last)
                for t in tiles(b):
                    last = dve.bn_aggr(mv[:, ln, t, :], stats[:, t, :])
                link(last)
                dve.tensor_scalar(vpe[:, ln, span(b)], mv[:, ln, span(b), 1], LN_EPS, None,
                                  ALU.add).then_inc(vpe_ready[ln], 1)

            def normalise(ln, b, into, source, scale):
                for t in tiles(b):
                    last = dve.tensor_scalar(into[:, t, :], source[:, t, :], mv[:, ln, t, 0:1],
                                             scale[:, t:t + 1], ALU.subtract, ALU.mult)
                return last

            def x_stats(b):
                dve.wait_ge(x_in[b], 16)
                statistics(LX, b, lambda i, t: x_tok[:, t, :])

            def x_norm(b):
                dve.wait_ge(rstd_ready[LX], b + 1)
                normalise(LX, b, xn_tok, x_tok, rstd[:, LX, :]).then_inc(xn_ready, 1)

            def layer1(b):
                dve.wait_ge(sig1_ready, b + 1)
                dve.scalar_tensor_tensor(out=cut(s1, b), in0=bank[4 + b % 2][:], scalar=col(B1),
                                         in1=cut(sig1, b), op0=ALU.add, op1=ALU.mult).then_inc(s1_done, 1)
                dve.wait_ge(s1_done, b + 1)
                dve.tensor_tensor(cut(h1T, b), cut(s1, b), cut(kT, b), ALU.add).then_inc(h1_done, 1)

            def layer2(b):
                dve.wait_ge(sig2_ready, b + 1)
                dve.scalar_tensor_tensor(out=cut(s2, b), in0=bank[b % 2][:], scalar=col(B2),
                                         in1=cut(sig2, b), op0=ALU.add, op1=ALU.mult).then_inc(s2_done, 1)
                dve.wait_ge(s2_done, b + 1)
                dve.wait_ge(hv_done, b + 1)
                dve.tensor_tensor(cut(hvT, b), cut(s2, b), cut(hvT, b), ALU.add).then_inc(e_done, 1)
                dve.scalar_tensor_tensor(out=cut(u2T, b), in0=cut(s2, b), scalar=1.0, in1=cut(sig2, b),
                                         op0=ALU.subtract, op1=ALU.mult).then_inc(u2_done, 1)
                dve.wait_ge(e_done, b + 1)
                dve.scalar_tensor_tensor(out=cut(dpT, b), in0=cut(hvT, b), scalar=GRAD_SCALE,
                                         in1=cut(alrT, b), op0=ALU.mult, op1=ALU.mult).then_inc(dp_done, 1)
                dve.scalar_tensor_tensor(out=cut(u1T, b), in0=cut(s1, b), scalar=1.0, in1=cut(sig1, b),
                                         op0=ALU.subtract, op1=ALU.mult).then_inc(u1_done, 1)
                dve.wait_ge(dp_done, b + 1)
                dve.wait_ge(d2_done, b + 1)
                dve.scalar_tensor_tensor(out=cut(dz2T, b), in0=cut(dpT, b), scalar=1.0, in1=cut(d2T, b),
                                         op0=ALU.mult, op1=ALU.mult,
                                         accum_out=gb[:, 1, b:b + 1]).then_inc(dz2_done, 1)

            def layer1_back(b):
                dve.wait_ge(dh1_mm, b + 1)
                dve.tensor_tensor(cut(dh1T, b), bank[6 + b % 2][:], cut(dpT, b), ALU.add).then_inc(dh1_done, 1)
                dve.wait_ge(dh1_done, b + 1)
                dve.wait_ge(d1_done, b + 1)
                dve.scalar_tensor_tensor(out=cut(dz1T, b), in0=cut(dh1T, b), scalar=1.0, in1=cut(d1T, b),
                                         op0=ALU.mult, op1=ALU.mult,
                                         accum_out=gb[:, 0, b:b + 1]).then_inc(dz1_done, 1)

            def adam(new, old, g, tmp, rcp):
                link(dve.tensor_scalar(tmp, g, -1.0, ADAM_EPS, ALU.mult, ALU.add))
                link(dve.scalar_tensor_tensor(out=tmp, in0=g, scalar=ADAM_EPS, in1=tmp, op0=ALU.add,
                                              op1=ALU.max))
                link(dve.reciprocal(rcp, tmp))
                link(dve.scalar_tensor_tensor(out=tmp, in0=g, scalar=-LR, in1=rcp, op0=ALU.mult, op1=ALU.mult))
                return dve.scalar_tensor_tensor(out=new, in0=old, scalar=1.0 - LR * WD, in1=tmp,
                                                op0=ALU.mult, op1=ALU.add)

            dve.memset(b2_stack[:], 0.0).then_inc(b2_zero, 1)
            x_stats(0)
            x_stats(1)
            x_norm(0)
            x_stats(2)
            x_norm(1)
            x_stats(3)
            x_norm(2)
            dve.wait_ge(cols_ready, 1)
            layer1(0)
            x_norm(3)
            for b in range(1, NB):
                layer1(b)
            for b in range(NB):
                layer2(b)
                if b:
                    layer1_back(b - 1)
            layer1_back(NB - 1)
            dve.wait_ge(gw2_mm, 1)
            adam(w2n[:], w2_sb[:], bank[5][:, 0:P], adam_tmp[:, 0, :], adam_tmp[:, 1, :]).then_inc(w2n_ready, 1)
            dve.wait_ge(dz1_done, NB)
            link(dve.tensor_reduce(gbs[:], gb[:], AX_X, ALU.add))
            adam(bn[:], cols[:, B1:B1 + 2], gbs[:], gb_tmp[:], gb[:, 0, 0:2]).then_inc(bn_ready, 1)
            dve.wait_ge(w2n_ready, 1)
            dve.wait_ge(gw1_mm, 1)
            adam(w1n[:], w1_sb[:], bank[1][:, 0:P], adam_tmp[:, 0, :], adam_tmp[:, 1, :]).then_inc(w1n_ready, 1)
            dve.wait_ge(bn_ready, 1)
            for b in range(NB):
                dve.wait_ge(rsig1_ready, b + 1)
                dve.scalar_tensor_tensor(out=cut(r_sig1, b), in0=bank[4 + b % 2][:], scalar=bn[:, 0:1],
                                         in1=cut(r_sig1, b), op0=ALU.add, op1=ALU.mult).then_inc(rs1_done, 1)
                dve.wait_ge(rs1_done, b + 1)
                dve.wait_ge(qT_ready, b + 1)
                dve.tensor_tensor(cut(r_h1T, b), cut(r_sig1, b), cut(qT, b), ALU.add).then_inc(rh1_done, 1)
            for b in range(NB):
                dve.wait_ge(rsig2_ready, b + 1)
                dve.scalar_tensor_tensor(out=cut(r_sig2, b), in0=bank[6 + b % 2][:], scalar=bn[:, 1:2],
                                         in1=cut(r_sig2, b), op0=ALU.add, op1=ALU.mult).then_inc(rs2_done, 1)
                dve.wait_ge(rs2_done, b + 1)
                dve.tensor_tensor(cut(rT, b), cut(r_sig2, b), cut(r_h1T, b), ALU.add).then_inc(r_done, 1)

            def minus_mean(ln, b, s):
                dve.wait_ge(rstd_ready[ln], b + 1)
                dve.scalar_tensor_tensor(out=nmean[:, ln, span(b)], in0=mv[:, ln, span(b), 0], scalar=-1.0,
                                         in1=rstd[:, ln, span(b)], op0=ALU.mult, op1=ALU.mult).then_inc(s, 1)

            for what, b in SCHEDULE:
                if what == "norm_r":
                    dve.wait_ge(r_tr, b + 1)
                    statistics(LR_, b, lambda i, t: bank[2 + b % 2][:, i * P:(i + 1) * P])
                if what == "center_r":
                    minus_mean(LR_, b, nmr_ready)
                if what == "norm_x1":
                    dve.wait_ge(rn_ready, b + 1)
                    link(dve.tensor_tensor(tok(x1_tok, b), tok(x1_tok, b), tok(x_tok, b), ALU.add))
                    statistics(L1, b, lambda i, t: x1_tok[:, t, :])
                if what == "norm_z":
                    minus_mean(L1, b, nm1_ready)
                    link(dve.tensor_tensor(r2[:, 0, span(b)], rstd[:, L1, span(b)], rstd[:, L1, span(b)], ALU.mult))
                    link(dve.tensor_tensor(r2[:, 1, span(b)], r2[:, 0, span(b)], mv[:, L1, span(b), 1], ALU.mult))
                    dve.tensor_scalar(vpe[:, LZ, span(b)], r2[:, 1, span(b)], LN_EPS, None,
                                      ALU.add).then_inc(vpe_ready[LZ], 1)
                if what == "scale_z":
                    dve.wait_ge(rstd_ready[LZ], b + 1)
                    link(dve.tensor_tensor(nmean[:, LZ, span(b)], rstd[:, L1, span(b)], rstd[:, LZ, span(b)],
                                           ALU.mult))
                    normalise(L1, b, zt_tok, x1_tok, nmean[:, LZ, :]).then_inc(zt_ready, 1)

            def wide(v):
                return v.unsqueeze(2).to_broadcast([P, T, E])

            mx, sm, rs, m1, f1, m2, f2, dn = (red[:, i, :] for i in range(8))
            dve.wait_ge(rb_in, 16)
            dve.wait_ge(ramp_ready, 1)
            dve.wait_ge(lg_mm, NB)
            dve.tensor_tensor(lg, bank[4][:, 0:T * E].rearrange("p (t e) -> p t e", e=E),
                              rb_b[:].unsqueeze(1).to_broadcast([P, T, E]), ALU.add).then_inc(lg_read, 1)
            dve.wait_ge(lg_read, 1)
            link(dve.tensor_reduce(mx, lg, AX_X, ALU.max))
            dve.tensor_tensor(lg, lg, wide(mx), ALU.subtract).then_inc(lg_shift, 1)
            for b in range(NB):
                dve.wait_ge(zhi_done, b + 1)
                dve.tensor_tensor(cut(z_lo, b), cut(zT, b), cut(z_hi, b).bitcast(F32),
                                  ALU.subtract).then_inc(zlo_done, 1)
            dve.wait_ge(ex_ready, 1)
            link(dve.tensor_reduce(sm, ex, AX_X, ALU.add))
            link(dve.reciprocal(rs, sm))
            link(dve.tensor_tensor(pr, ex, wide(rs), ALU.mult))

            def first_largest(source, most, rank, onehot):
                link(dve.tensor_reduce(most, source, AX_X, ALU.max))
                link(dve.tensor_tensor(eq, source, wide(most), ALU.is_equal))
                link(dve.tensor_tensor(eq, eq, ramp[:], ALU.mult))
                link(dve.tensor_reduce(rank, eq, AX_X, ALU.max))
                link(dve.tensor_tensor(onehot, eq, wide(rank), ALU.is_equal))

            first_largest(pr, m1, f1, oh1)
            link(dve.scalar_tensor_tensor(out=ex, in0=oh1, scalar=-2.0, in1=pr,
                                          op0=ALU.mult, op1=ALU.add))
            first_largest(ex, m2, f2, oh2)
            link(dve.tensor_tensor(dn, m1, m2, ALU.add))
            link(dve.tensor_scalar(dn, dn, 1e-8, None, ALU.max))
            link(dve.reciprocal(rs, dn))
            link(dve.tensor_tensor(oh1, oh1, oh2, ALU.add))
            link(dve.tensor_tensor(oh1, oh1, pr, ALU.mult))
            link(dve.tensor_tensor(pr, oh1, wide(rs), ALU.mult))
            link(dve.tensor_copy(w_hi[:], pr))
            dve.wait_ge(wpad_zero, 1)
            link(dve.tensor_copy(w_pad[:, :, 0:E], w_hi[:].bitcast(F32)))
            dve.tensor_tensor(w_pad[:, :, E:2 * E], pr, w_hi[:].bitcast(F32), ALU.subtract).then_inc(w_ready, 1)

            def weigh(j, i):
                dve.wait_ge(g_done, j * UB + (i + 1))
                if i % C == 0:
                    dve.wait_ge(wb_mm, j * E + (i // C + 1))
                dve.tensor_tensor(t_buf[i % RING], g_buf[i % RING], bank[2 + i // C % 2][:],
                                  ALU.mult).then_inc(t_done, 1)

            def lo(j, i):
                dve.wait_ge(hi_done, j * UB + (i + 1))
                dve.tensor_tensor(lo_buf[i % RING][:], t_buf[i % RING], hi_buf[i % RING][:].bitcast(F32),
                                  ALU.subtract).then_inc(lo_done, 1)

            def y_stats(b):
                dve.wait_ge(o_tr, b + 1)
                dve.wait_ge(u_ready, b + 1)
                dve.tensor_tensor(tok(y_tok, b), bank3(5), tok(u_tok, b), ALU.add).then_inc(y_ready, 1)
                dve.wait_ge(y_ready, b + 1)
                statistics(LY, b, lambda i, t: y_tok[:, t, :])

            def y_norm(b):
                dve.wait_ge(rstd_ready[LY], b + 1)
                link(normalise(LY, b, y_tok, y_tok, rstd[:, LY, :]))
                dve.tensor_tensor(tok(x1_tok, b), tok(x1_tok, b), tok(y_tok, b), ALU.add).then_inc(yn_done, 1)

            weigh(0, 0)
            weigh(0, 1)
            lo(0, 0)

            def body(j, last):
                for i in range(UB):
                    ahead(weigh, j, i + T_AHEAD, last)
                    ahead(lo, j, i + LO_AHEAD, last)
                    if last and i in EPILOGUE:
                        y_stats(EPILOGUE[i])
                    if last and i - 2 in EPILOGUE:
                        y_norm(EPILOGUE[i - 2])

            with dve.Fori(0, NB - 1) as j:
                body(j, False)
            body(NB - 1, True)
            y_stats(NB - 1)
            y_norm(NB - 1)


_INS = ['L0_attn_x', 'L0_attn_Wk', 'L0_attn_bk', 'L0_attn_Wq', 'L0_attn_bq', 'L0_attn_Wv', 'L0_attn_bv',
        'L0_attn_Wlr', 'L0_attn_blr', 'L0_attn_W1', 'L0_attn_b1', 'L0_attn_W2', 'L0_attn_b2',
        'L0_ffn_ln_g', 'L0_ffn_ln_b', 'L0_ffn_rW', 'L0_ffn_rb', 'L0_ffn_W1', 'L0_ffn_b1', 'L0_ffn_W2',
        'L0_ffn_b2']
_OUTS = [((8, 256, 128), 'float32')]


def kernel(**inputs):
    import numpy as _np
    import concourse.bacc as _bacc
    from concourse import mybir as _mybir
    from concourse.bass_utils import run_bass_kernel_spmd as _run

    nc = _bacc.Bacc("TRN2", target_bir_lowering=False, num_devices=1)
    arrays, args = {}, []
    for name in _INS:
        a = _np.ascontiguousarray(inputs[name])
        arrays[f"in_{name}_dram"] = a
        args.append(nc.dram_tensor(f"in_{name}_dram", a.shape, _mybir.dt.from_np(a.dtype), kind="ExternalInput").ap())
    for i, (shape, dtype) in enumerate(_OUTS):
        dt = _mybir.dt.from_np(_np.dtype(dtype))
        args.append(nc.dram_tensor(f"out_{i}_dram", shape, dt, kind="ExternalOutput").ap())
    memory_and_experts(nc, *args)
    r = _run(nc, [arrays], core_ids=[0])
    return r.results[0]["out_0_dram"]
```

```python
from contextlib import ExitStack

import concourse.bass as bass
from concourse import mybir

ALU = mybir.AluOpType
ACT = mybir.ActivationFunctionType
AX_X = mybir.AxisListType.X
F32 = mybir.dt.float32
F32R = mybir.dt.float32r
ENG = mybir.EngineType

P = 128
BLOCK = 512
LN_EPS = 1e-5
LR = 0.01
WD = 0.01
MAX_ALR = 0.1
ADAM_EPS = 1e-8


def memory_and_experts(nc, x, Wk, bk, Wq, bq, Wv, bv, Wlr, blr, W1, b1, W2, b2,
                       ln_g, ln_b, rW, rb, fW1, fb1, fW2, fb2, out):
    B, S, D = x.shape
    E, H, HF = fW1.shape
    N = B * S
    T = N // P
    NB = N // BLOCK
    TB = BLOCK // P
    C = HF // P
    assert D == P and H == P and T == NB * TB
    UNITS = NB * E * C
    UB = E * C
    GRAD_SCALE = 2.0 * MAX_ALR / D

    x_v = x.rearrange("b s d -> (b s) d").rearrange("(p t) d -> p t d", p=P)
    out_v = out.rearrange("b s d -> (b s) d").rearrange("(p t) d -> p t d", p=P)

    with ExitStack() as ctx:
        def sb(name, shape, dt=F32):
            return ctx.enter_context(nc.sbuf_tensor(name, shape, dt))

        def sem(name):
            return ctx.enter_context(nc.semaphore(name))

        bank = [ctx.enter_context(nc.psum_tensor(f"bank{i}", [P, BLOCK], F32)) for i in range(8)]

        x_tok = sb("x_tok", [P, T, D])
        xn_tok = sb("xn_tok", [P, T, D])
        x1_tok = xn_tok
        xnT = sb("xnT", [P, N])
        kT = sb("kT", [P, N])
        vT = sb("vT", [P, N])
        sig1 = sb("sig1", [P, N])
        s1 = sb("s1", [P, N])
        h1T = sb("h1T", [P, N])
        sig2 = sb("sig2", [P, N])
        s2 = sb("s2", [P, N])
        alrT = sb("alrT", [P, N])
        qT = sb("qT", [P, N])
        k_tok = sb("k_tok", [P, T, D])
        h1_tok = sb("h1_tok", [P, T, D])
        dz2_tok = kT[:].rearrange("p (t d) -> p t d", d=D)
        dz1_tok = h1T[:].rearrange("p (t d) -> p t d", d=D)
        hvT, dh1T = vT, vT
        dpT = alrT
        u2T, dz2T = sig2, sig2
        d2T = s2
        u1T, dz1T = sig1, sig1
        d1T = s1
        r_sig1, r_h1T, r_sig2, rT = s1, xnT, s2, vT
        zT = alrT
        zt_tok = h1_tok
        w_pad = qT[:].rearrange("p (t d) -> p t d", d=P)
        z_hi = sb("z_hi", [P, N], F32R)
        z_lo = sb("z_lo", [P, N], F32R)
        wT = sb("wT", [P, N], F32R)
        fW_raw = sb("fW_raw", [P, E * HF])
        fW1_hi = sb("fW1_hi", [P, E * HF], F32R)
        fW1_lo = sb("fW1_lo", [P, E * HF], F32R)
        fW2_hi = sb("fW2_hi", [P, E * C * H], F32R)
        fW2_lo = sb("fW2_lo", [P, E * C * H], F32R)
        sel = sb("sel", [P, E], F32R)
        RING, SPLIT_RING = 6, 5
        dead = [tensor[:, i * BLOCK:(i + 1) * BLOCK] for tensor in (sig1, s1, sig2) for i in range(4)]
        g_buf, t_buf = dead[:RING], dead[RING:]
        oT = s2
        y_tok = xnT[:].rearrange("p (t d) -> p t d", d=D)
        hi_buf = [sb(f"hi_buf{i}", [P, BLOCK], F32R) for i in range(SPLIT_RING)]
        lo_buf = [sb(f"lo_buf{i}", [P, BLOCK], F32R) for i in range(SPLIT_RING)]

        ident = sb("ident", [P, P])
        NV = 7 + E * C
        rows = sb("rows", [NV, P])
        cols = sb("cols", [P, NV])
        BK, BQ, BV, B1, B2, G, BB, FB1 = range(8)
        wk_sb, wq_sb, wv_sb = (sb(n, [P, P]) for n in ("wk_sb", "wq_sb", "wv_sb"))
        wlr_sb = sb("wlr_sb", [P, 1])
        wlr_b = sb("wlr_b", [P, P])
        blr_b = sb("blr_b", [P, 1])
        w1_sb, w2_sb, w2T_sb = (sb(n, [P, P]) for n in ("w1_sb", "w2_sb", "w2T_sb"))
        w1n, w2n = sb("w1n", [P, P]), sb("w2n", [P, P])
        adam_tmp = sb("adam_tmp", [P, 2, P])
        gb = sb("gb", [P, 2, NB])
        gbs = sb("gbs", [P, 2])
        gb_tmp = sb("gb_tmp", [P, 2])
        bn = sb("bn", [P, 2])
        rw_sb = sb("rw_sb", [P, E])
        rb_b = sb("rb_b", [P, E])
        b2_stack = sb("b2_stack", [P, H])
        b2_hi = sb("b2_hi", [P, H], F32R)
        b2_lo = sb("b2_lo", [P, H], F32R)
        stats = sb("stats", [P, T, 6])
        LX, LR_, L1, LZ, LY = range(5)
        mv = sb("mv", [P, 5, T, 2])
        vpe = sb("vpe", [P, 5, T])
        rstd = sb("rstd", [P, 5, T])
        shift = sb("shift", [P, 2, T])
        minus_half = sb("minus_half", [P, TB])
        ramp = sb("ramp", [P, TB, E])
        lg, ex, pr, eq, oh1, oh2 = (kT[:, i * T * E:(i + 1) * T * E].rearrange("p (t e) -> p t e", e=E)
                                    for i in range(6))
        w_hi = sb("w_hi", [P, T, E], F32R)
        red = kT[:, 6 * T * E:7 * T * E].rearrange("p (i t) -> p i t", t=T)

        x_in = [sem(f"x_in{i}") for i in range(NB)]
        rows_in, wk_in, wq_in, wv_in, wlr_in, blr_in = (sem(n) for n in (
            "rows_in", "wk_in", "wq_in", "wv_in", "wlr_in", "blr_in"))
        w1_in, w2_in, rw_in, rb_in, fw1_in, fw2_in, b2s_in = (sem(n) for n in (
            "w1_in", "w2_in", "rw_in", "rb_in", "fw1_in", "fw2_in", "b2s_in"))
        out_done = sem("out_done")
        zeroed, ident_ready, half_ready, ramp_ready, wpad_zero, b2_zero = (sem(n) for n in (
            "zeroed", "ident_ready", "half_ready", "ramp_ready", "wpad_zero", "b2_zero"))
        wlrb_ready, sel_ready, fw_hi_done, fw_lo_done, b2hi_done, b2lo_done = (sem(n) for n in (
            "wlrb_ready", "sel_ready", "fw_hi_done", "fw_lo_done", "b2hi_done", "b2lo_done"))
        dve_step = sem("dve_step")
        vpe_ready = [sem(f"vpe_ready{i}") for i in range(5)]
        rstd_ready = [sem(f"rstd_ready{i}") for i in range(5)]
        xn_ready, vecs_tr, cols_ready, w2T_tr, w2T_ready = (sem(n) for n in (
            "xn_ready", "vecs_tr", "cols_ready", "w2T_tr", "w2T_ready"))
        xn_tr, xnT_ready, k_mm, kT_ready, v_mm, vT_ready, z1_mm, sig1_ready = (sem(n) for n in (
            "xn_tr", "xnT_ready", "k_mm", "kT_ready", "v_mm", "vT_ready", "z1_mm", "sig1_ready"))
        s1_done, h1_done, hv_done, alr_mm, alr_ready, z2_mm, sig2_ready, s2_done = (sem(n) for n in (
            "s1_done", "h1_done", "hv_done", "alr_mm", "alr_ready", "z2_mm", "sig2_ready", "s2_done"))
        e_done, u2_done, d2_done, dz2_done, dh1_mm, dh1_done, u1_done, d1_done, dz1_done = (
            sem(n) for n in ("e_done", "u2_done", "d2_done", "dz2_done", "dh1_mm", "dh1_done",
                             "u1_done", "d1_done", "dz1_done"))
        tok_tr, tok_out, q_mm, qT_ready, gw2_mm, gw1_mm, w2n_ready, w1n_ready, bn_ready = (
            sem(n) for n in ("tok_tr", "tok_out", "q_mm", "qT_ready", "gw2_mm", "gw1_mm",
                             "w2n_ready", "w1n_ready", "bn_ready"))
        rz1_mm, rsig1_ready, rh1_done, rz2_mm, rsig2_ready, r_done, r_tr = (sem(n) for n in (
            "rz1_mm", "rsig1_ready", "rh1_done", "rz2_mm", "rsig2_ready", "r_done", "r_tr"))
        x1_ready, zt_ready, zt_tr, zT_ready, zhi_done, zlo_done = (
            sem(n) for n in ("x1_ready", "zt_ready", "zt_tr",
                             "zT_ready", "zhi_done", "zlo_done"))
        lg_mm, lg_shift, ex_ready, w_ready, w_tr, wT_ready = (sem(n) for n in (
            "lg_mm", "lg_shift", "ex_ready", "w_ready", "w_tr", "wT_ready"))
        rs1_done, rs2_done, shift_ready, lg_read, dp_done = (sem(n) for n in (
            "rs1_done", "rs2_done", "shift_ready", "lg_read", "dp_done"))
        h_mm, g_done, wb_mm, t_done, hi_done, lo_done, y_mm = (sem(n) for n in (
            "h_mm", "g_done", "wb_mm", "t_done", "hi_done", "lo_done", "y_mm"))
        oT_ready, o_tr, y_ready, yn_done = (sem(n) for n in (
            "oT_ready", "o_tr", "y_ready", "yn_done"))

        Y_TR, Y_STATS, Y_NORM = 1, 2, 5
        ROUTER, ROUTER_STEPS, EXP, EXP_PIECES, W_TR = 0, 3, 1, 6, 11
        R_TR, NORM_R, RESIDUAL, NORM_Z, Z_TR, Z_LOW = 3, 5, 8, 11, 13, 14

        RZ1, RZ2 = (0, 1, 2, 0), (3, 5, 6, 1)

        H_AHEAD, WB_AHEAD, T_AHEAD, HI_AHEAD, LO_AHEAD = 5, 4, 3, 3, 2

        def tiles(b):
            return range(TB * b, TB * b + TB)

        def cut(tensor, b):
            return tensor[:, b * BLOCK:(b + 1) * BLOCK]

        def tok(tensor, b):
            return tensor[:, TB * b:TB * b + TB, :]

        def col(i):
            return cols[:, i:i + 1]

        def bank3(i):
            return bank[i][:].rearrange("p (t d) -> p t d", d=P)

        block = ctx.enter_context(nc.Block())

        @block.sync
        def _(sp):
            for b in range(NB):
                sp.dma_start(tok(x_tok, b), tok(x_v, b)).then_inc(x_in[b], 16)
            sp.dma_start(wk_sb[:], Wk).then_inc(wk_in, 16)
            sp.dma_start(wv_sb[:], Wv).then_inc(wv_in, 16)
            sp.dma_start(w1_sb[:], W1).then_inc(w1_in, 16)
            sp.dma_start(w2_sb[:], W2).then_inc(w2_in, 16)
            sp.dma_start(wq_sb[:], Wq).then_inc(wq_in, 16)
            sp.dma_start(fW_raw[:].rearrange("p (e f) -> p e f", f=HF),
                         fW1.rearrange("e h f -> h e f")).then_inc(fw1_in, 16)
            sp.wait_ge(fw_lo_done, 1)
            sp.dma_start(fW_raw[:].rearrange("p (e h) -> p e h", h=H),
                         fW2.rearrange("e (c f) h -> f (e c) h", f=P)).then_inc(fw2_in, 16)
            for b in range(NB):
                sp.wait_ge(yn_done, b + 1)
                sp.dma_start(tok(out_v, b), tok(x1_tok, b)).then_inc(out_done, 16)
            sp.wait_ge(out_done, 16 * NB)

        @block.gpsimd
        def _(pool):
            pool.memset(ident[:], 0.0).then_inc(zeroed, 1)
            pool.wait_ge(zeroed, 1)
            pool.affine_select(out=ident[:], in_=ident[:], compare_op=ALU.not_equal, fill=1.0, base=0,
                               pattern=[[-1, P]], channel_multiplier=1).then_inc(ident_ready, 1)
            pool.memset(minus_half[:], -0.5).then_inc(half_ready, 1)
            pool.wait_ge(half_ready, 1)

            def rsqrt(ln, b):
                pool.wait_ge(vpe_ready[ln], b + 1)
                pool.tensor_tensor(rstd[:, ln, TB * b:TB * b + TB], vpe[:, ln, TB * b:TB * b + TB],
                                   minus_half[:], ALU.pow).then_inc(rstd_ready[ln], 1)

            rsqrt(LX, 0)
            rsqrt(LX, 1)
            pool.wait_ge(wlr_in, 16)
            pool.tensor_scalar(wlr_b[:], wlr_sb[:].to_broadcast([P, P]), 1.0, 0.0, ALU.mult,
                               ALU.add).then_inc(wlrb_ready, 1)
            rsqrt(LX, 2)
            rsqrt(LX, 3)
            pool.iota(ramp[:], pattern=[[0, TB], [-1, E]], base=E, channel_multiplier=0,
                      allow_small_or_imprecise_dtypes=True).then_inc(ramp_ready, 1)

            def split_weights(n, loaded, hi, lo):
                pool.wait_ge(loaded, 16)
                pool.tensor_scalar(hi[:], fW_raw[:], 1.0, 0.0, ALU.mult, ALU.add).then_inc(fw_hi_done, 1)
                pool.wait_ge(fw_hi_done, n)
                pool.tensor_tensor(lo[:], fW_raw[:], hi[:].bitcast(F32), ALU.subtract).then_inc(fw_lo_done, 1)

            split_weights(1, fw1_in, fW1_hi, fW1_lo)
            for b in range(NB):
                pool.wait_ge(h1_done, b + 1)
                pool.wait_ge(vT_ready, b + 1)
                pool.tensor_tensor(cut(hvT, b), cut(h1T, b), cut(vT, b), ALU.subtract).then_inc(hv_done, 1)
            for b in range(NB):
                pool.wait_ge(u2_done, b + 1)
                pool.tensor_tensor(cut(d2T, b), cut(s2, b), cut(u2T, b), ALU.subtract).then_inc(d2_done, 1)
                pool.wait_ge(u1_done, b + 1)
                pool.tensor_tensor(cut(d1T, b), cut(s1, b), cut(u1T, b), ALU.subtract).then_inc(d1_done, 1)
            split_weights(2, fw2_in, fW2_hi, fW2_lo)
            pool.wait_ge(ident_ready, 1)
            pool.tensor_tensor(sel[:], ident[:, 0:E], ident[:, E:2 * E], ALU.add).then_inc(sel_ready, 1)
            pool.wait_ge(b2s_in, 32)
            pool.tensor_scalar(b2_hi[:], b2_stack[:], 1.0, 0.0, ALU.mult, ALU.add).then_inc(b2hi_done, 1)
            pool.wait_ge(b2hi_done, 1)
            pool.tensor_tensor(b2_lo[:], b2_stack[:], b2_hi[:].bitcast(F32),
                               ALU.subtract).then_inc(b2lo_done, 1)

            def clear_w(b):
                pool.wait_ge(rh1_done, b + 1)
                pool.memset(w_pad[:, TB * b:TB * b + TB, :], 0.0).then_inc(wpad_zero, 1)

            clear_w(0)
            clear_w(1)
            rsqrt(LR_, 0)
            clear_w(2)
            rsqrt(LZ, 0)
            rsqrt(L1, 0)
            clear_w(3)
            rsqrt(LR_, 1)
            rsqrt(LZ, 1)
            rsqrt(L1, 1)

            def lo(n):
                pool.wait_ge(hi_done, n + 1)
                pool.tensor_tensor(lo_buf[n % SPLIT_RING][:], t_buf[n % RING], hi_buf[n % SPLIT_RING][:].bitcast(F32),
                                   ALU.subtract).then_inc(lo_done, 1)

            for n in range(LO_AHEAD):
                lo(n)
            for j in range(NB):
                for i in range(UB):
                    n = j * UB + i
                    if n + LO_AHEAD < UNITS:
                        lo(n + LO_AHEAD)
                    if i == Y_STATS + 1 and j:
                        rsqrt(LY, j - 1)
                    if j + 2 < NB:
                        if i == NORM_R + 1:
                            rsqrt(LR_, j + 2)
                        if i == RESIDUAL + 2:
                            rsqrt(LZ, j + 2)
                            rsqrt(L1, j + 2)
            rsqrt(LY, NB - 1)

        @block.tensor
        def _(pe):
            def mm(out_, lhsT, rhs, start=True, stop=True):
                return pe.matmul(out_, lhsT, rhs, start=start, stop=stop)

            pe.wait_ge(ident_ready, 1)
            pe.wait_ge(rows_in, 16 * 8)
            pe.transpose(bank[7][:, 0:NV], rows[:, :], ident[0:NV, 0:NV]).then_inc(vecs_tr, 1)
            pe.wait_ge(w2_in, 16)
            pe.transpose(bank[7][:, P:2 * P], w2_sb[:], ident[:]).then_inc(w2T_tr, 1)

            def xn_transpose(b):
                pe.wait_ge(xn_ready, b + 1)
                if b >= 2:
                    pe.wait_ge(xnT_ready, b - 1)
                for i, t in enumerate(tiles(b)):
                    last = pe.transpose(bank[b % 2][:, i * P:(i + 1) * P], xn_tok[:, t, :], ident[:])
                last.then_inc(xn_tr, 1)

            def k_product(b):
                pe.wait_ge(wk_in, 16)
                pe.wait_ge(xnT_ready, b + 1)
                if b:
                    pe.wait_ge(kT_ready, b)
                mm(bank[2][:], wk_sb[:], cut(xnT, b)).then_inc(k_mm, 1)

            def v_product(b):
                pe.wait_ge(wv_in, 16)
                if b:
                    pe.wait_ge(vT_ready, b)
                mm(bank[3][:], wv_sb[:], cut(xnT, b)).then_inc(v_mm, 1)

            def z1_product(b):
                pe.wait_ge(w1_in, 16)
                pe.wait_ge(kT_ready, b + 1)
                if b >= 2:
                    pe.wait_ge(sig1_ready, b - 1)
                    pe.wait_ge(s1_done, b - 1)
                mm(bank[4 + b % 2][:], w1_sb[:], cut(kT, b)).then_inc(z1_mm, 1)

            def alr_product(b):
                pe.wait_ge(wlrb_ready, 1)
                if b == 1:
                    pe.wait_ge(cols_ready, 1)
                    pe.wait_ge(w2T_ready, 1)
                if b >= 2:
                    pe.wait_ge(alr_ready, b - 1)
                mm(bank[6 + b % 2][:], wlr_b[:], cut(xnT, b)).then_inc(alr_mm, 1)

            def z2_product(b):
                pe.wait_ge(h1_done, b + 1)
                if b < 2:
                    pe.wait_ge(xnT_ready, b + 3)
                else:
                    pe.wait_ge(sig2_ready, b - 1)
                    pe.wait_ge(s2_done, b - 1)
                mm(bank[b % 2][:], w2_sb[:], cut(h1T, b)).then_inc(z2_mm, 1)

            def token_major(n, source, b, ready, count):
                pe.wait_ge(ready, count)
                if n == 0:
                    pe.wait_ge(kT_ready, NB)
                elif n == 1:
                    pe.wait_ge(vT_ready, NB)
                else:
                    pe.wait_ge(tok_out, n - 1)
                for i in range(TB):
                    last = pe.transpose(bank[2 + n % 2][:, i * P:(i + 1) * P],
                                        source[:, b * BLOCK + i * P:b * BLOCK + (i + 1) * P], ident[:])
                last.then_inc(tok_tr, 1)

            def q_product(b):
                pe.wait_ge(wq_in, 16)
                if b:
                    pe.wait_ge(qT_ready, b)
                mm(bank[4][:], wq_sb[:], cut(xnT, b)).then_inc(q_mm, 1)

            def dh1_product(b):
                pe.wait_ge(w2T_ready, 1)
                pe.wait_ge(dz2_done, b + 1)
                if b < 2:
                    pe.wait_ge(alr_ready, b + 3)
                else:
                    pe.wait_ge(dh1_done, b - 1)
                mm(bank[6 + b % 2][:], w2T_sb[:], cut(dz2T, b)).then_inc(dh1_mm, 1)

            def gradient(into, left, right, b, out_count, done):
                pe.wait_ge(tok_out, out_count)
                for t in tiles(b):
                    last = mm(into, left[:, t, :], right[:, t, :], start=(t == 0), stop=(t == T - 1))
                if b == NB - 1:
                    last.then_inc(done, 1)

            xn_transpose(0)
            k_product(0)
            xn_transpose(1)
            v_product(0)
            for b in range(1, NB):
                z1_product(b - 1)
                k_product(b)
                if b + 1 < NB:
                    xn_transpose(b + 1)
                v_product(b)
            z1_product(NB - 1)
            for b in range(NB):
                alr_product(b)
                z2_product(b)
            for b in range(NB):
                token_major(2 * b, kT, b, kT_ready, b + 1)
                token_major(2 * b + 1, h1T, b, h1_done, b + 1)
            pe.wait_ge(sig1_ready, NB)
            pe.wait_ge(s1_done, NB)
            q_product(0)
            for b in range(NB):
                dh1_product(b)
                token_major(2 * NB + b, dz2T, b, dz2_done, b + 1)
                if b + 1 < NB:
                    q_product(b + 1)
                gradient(bank[5][:, 0:P], h1_tok, dz2_tok, b, 2 * NB + b + 1, gw2_mm)
            pe.wait_ge(s2_done, NB)
            for b in range(NB):
                token_major(3 * NB + b, dz1T, b, dz1_done, b + 1)
            for b in range(NB):
                gradient(bank[1][:, 0:P], k_tok, dz1_tok, b, 3 * NB + b + 1, gw1_mm)

            def rz1_product(b):
                if b == 0:
                    pe.wait_ge(w1n_ready, 1)
                    pe.wait_ge(qT_ready, NB)
                if b == NB - 1:
                    pe.wait_ge(rs1_done, 1)
                mm(bank[RZ1[b]][:], w1n[:], cut(qT, b)).then_inc(rz1_mm, 1)

            def rz2_product(b):
                pe.wait_ge(rh1_done, b + 1)
                if b == 0:
                    pe.wait_ge(w2n_ready, 1)
                    pe.wait_ge(tok_out, 4 * NB)
                if b == NB - 1:
                    pe.wait_ge(rs1_done, 2)
                mm(bank[RZ2[b]][:], w2n[:], cut(r_h1T, b)).then_inc(rz2_mm, 1)

            def r_transpose(b):
                pe.wait_ge(r_done, b + 1)
                if b:
                    pe.wait_ge(lg_read, b)
                for i in range(TB):
                    last = pe.transpose(bank[4][:, i * P:(i + 1) * P],
                                        rT[:, b * BLOCK + i * P:b * BLOCK + (i + 1) * P], ident[:])
                last.then_inc(r_tr, 1)

            def z_transpose(b):
                pe.wait_ge(zt_ready, b + 1)
                if b:
                    pe.wait_ge(zhi_done, b)
                else:
                    pe.wait_ge(dh1_done, NB)
                for i, t in enumerate(tiles(b)):
                    last = pe.transpose(bank[7][:, i * P:(i + 1) * P], zt_tok[:, t, :], ident[:])
                last.then_inc(zt_tr, 1)

            def logits(b):
                pe.wait_ge(zT_ready, b + 1)
                pe.wait_ge(x1_ready, b + 1)
                if b == 0:
                    pe.wait_ge(rw_in, 16)
                for i, t in enumerate(tiles(b)):
                    last = mm(bank[4][:, i * E:(i + 1) * E], zT[:, t * P:(t + 1) * P], rw_sb[:])
                last.then_inc(lg_mm, 1)

            def w_transpose(b):
                pe.wait_ge(w_ready, b + 1)
                if b >= 2:
                    pe.wait_ge(y_ready, b - 1)
                elif b:
                    pe.wait_ge(wT_ready, b)
                for i, t in enumerate(tiles(b)):
                    last = pe.transpose(bank[5][:, i * P:(i + 1) * P], w_pad[:, t, :], ident[:])
                last.then_inc(w_tr, 1)

            rz1_product(0)
            rz1_product(1)
            rz2_product(0)
            rz1_product(2)
            r_transpose(0)
            rz2_product(1)
            rz1_product(3)
            rz2_product(2)
            rz2_product(3)
            z_transpose(0)
            logits(0)
            r_transpose(1)

            def product3(into, w_hi, w_lo, a_hi, a_lo, start, stop):
                mm(into, w_hi, a_hi, start=start, stop=False)
                mm(into, w_lo, a_hi, start=False, stop=False)
                return mm(into, w_hi, a_lo, start=False, stop=stop)

            def weights(n):
                j, i = divmod(n, UB)
                e = i // C
                pe.wait_ge(wT_ready, j + 1)
                if n >= 2 * C:
                    pe.wait_ge(t_done, n - C)
                mm(bank[2 + e % 2][:], sel[:, e:e + 1].to_broadcast([P, P]), cut(wT, j)).then_inc(wb_mm, 1)

            def hidden(n):
                j, i = divmod(n, UB)
                s = slice(i * P, (i + 1) * P)
                if i == 0:
                    pe.wait_ge(zhi_done, j + 1)
                    pe.wait_ge(zlo_done, j + 1)
                if n >= 2:
                    pe.wait_ge(g_done, n - 1)
                product3(bank[n % 2][:], fW1_hi[:, s], fW1_lo[:, s], cut(z_hi, j), cut(z_lo, j),
                         True, True).then_inc(h_mm, 1)

            def output(n):
                i = n % UB
                s = slice(i * H, (i + 1) * H)
                pe.wait_ge(lo_done, n + 1)
                product3(bank[6][:], fW2_hi[:, s], fW2_lo[:, s], hi_buf[n % SPLIT_RING][:], lo_buf[n % SPLIT_RING][:],
                         False, i == UB - 1).then_inc(y_mm, 1)

            def bias_term(j):
                if j:
                    pe.wait_ge(oT_ready, j)
                mm(bank[6][:], b2_hi[:], cut(wT, j), start=True, stop=False)
                mm(bank[6][:], b2_lo[:], cut(wT, j), start=False, stop=False)

            def final_transpose(b):
                pe.wait_ge(oT_ready, b + 1)
                pe.wait_ge(wT_ready, min(b + 2, NB))
                if b == NB - 1:
                    pe.wait_ge(y_ready, b)
                for i in range(TB):
                    last = pe.transpose(bank[5][:, i * P:(i + 1) * P],
                                        oT[:, b * BLOCK + i * P:b * BLOCK + (i + 1) * P], ident[:])
                last.then_inc(o_tr, 1)

            pe.wait_ge(fw_hi_done, 2)
            pe.wait_ge(fw_lo_done, 2)
            pe.wait_ge(rs1_done, NB)
            pe.wait_ge(rs2_done, NB)
            for n in range(4):
                hidden(n)
            w_transpose(0)
            pe.wait_ge(sel_ready, 1)
            pe.wait_ge(b2lo_done, 1)
            weights(0)
            weights(C)
            z_transpose(1)
            hidden(4)
            bias_term(0)
            logits(1)
            for j in range(NB):
                for i in range(UB):
                    n = j * UB + i
                    if n + H_AHEAD < UNITS:
                        hidden(n + H_AHEAD)
                    if n + WB_AHEAD < UNITS and (n + WB_AHEAD) % C == 0:
                        weights(n + WB_AHEAD)
                    if i == 0 and j:
                        bias_term(j)
                    output(n)
                    if i == Y_TR and j:
                        final_transpose(j - 1)
                    if i == R_TR and j + 2 < NB:
                        r_transpose(j + 2)
                    if i == Z_TR and j + 2 < NB:
                        z_transpose(j + 2)
                    if i == W_TR and j + 1 < NB:
                        w_transpose(j + 1)
                    if i == Z_TR + 1 and j + 2 < NB:
                        logits(j + 2)
            final_transpose(NB - 1)

        @block.scalar
        def _(act):
            def dma(dst, src, s):
                act.dma_start(dst, src).then_inc(s, 16)

            def row(v):
                return v.rearrange("(a d) -> a d", a=1)

            for i, v in enumerate((bk, bq, bv, b1, b2, ln_g, ln_b)):
                dma(rows[i:i + 1, :], row(v), rows_in)
            dma(rows[7:NV, :], fb1.rearrange("e (c f) -> (e c) f", f=P), rows_in)
            dma(wlr_sb[:], Wlr, wlr_in)
            dma(blr_b[:], row(blr).to_broadcast([P, 1]), blr_in)
            dma(rw_sb[:], rW, rw_in)
            dma(rb_b[:], row(rb).to_broadcast([P, E]), rb_in)
            act.wait_ge(b2_zero, 1)
            for i in range(2):
                dma(b2_stack[i * E:(i + 1) * E, :], fb2, b2s_in)

            def copy(dst, src, s, **kw):
                act.activation(dst, src, ACT.Identity, **kw).then_inc(s, 1)

            act.wait_ge(vecs_tr, 1)
            act.wait_ge(w2T_tr, 1)
            copy(cols[:], bank[7][:, 0:NV], cols_ready)
            act.wait_ge(cols_ready, 1)
            copy(w2T_sb[:], bank[7][:, P:2 * P], w2T_ready)

            def xnT_out(b):
                act.wait_ge(xn_tr, b + 1)
                copy(cut(xnT, b), bank[b % 2][:], xnT_ready)

            def kT_out(b):
                act.wait_ge(k_mm, b + 1)
                copy(cut(kT, b), bank[2][:], kT_ready, bias=col(BK))

            def vT_out(b):
                act.wait_ge(v_mm, b + 1)
                copy(cut(vT, b), bank[3][:], vT_ready, bias=col(BV))

            def sigmoid(b, product, count, source, into, bias, s):
                act.wait_ge(product, count)
                act.activation(cut(into, b), source[:], ACT.Sigmoid, bias=bias).then_inc(s, 1)

            def sig1_out(b):
                sigmoid(b, z1_mm, b + 1, bank[4 + b % 2], sig1, col(B1), sig1_ready)

            xnT_out(0)
            kT_out(0)
            xnT_out(1)
            vT_out(0)
            for b in range(1, NB):
                sig1_out(b - 1)
                kT_out(b)
                if b + 1 < NB:
                    xnT_out(b + 1)
                vT_out(b)
            sig1_out(NB - 1)
            act.wait_ge(blr_in, 16)
            for b in range(NB):
                sigmoid(b, alr_mm, b + 1, bank[6 + b % 2], alrT, blr_b[:], alr_ready)
                sigmoid(b, z2_mm, b + 1, bank[b % 2], sig2, col(B2), sig2_ready)

            def token_major_out(n, into, b):
                act.wait_ge(tok_tr, n + 1)
                act.activation(tok(into, b), bank3(2 + n % 2), ACT.Identity).then_inc(tok_out, 1)

            def qT_out(b):
                act.wait_ge(q_mm, b + 1)
                copy(cut(qT, b), bank[4][:], qT_ready, bias=col(BQ))

            for b in range(NB):
                token_major_out(2 * b, k_tok, b)
                token_major_out(2 * b + 1, h1_tok, b)
            qT_out(0)
            for b in range(NB):
                token_major_out(2 * NB + b, dz2_tok, b)
                if b + 1 < NB:
                    qT_out(b + 1)
            for b in range(NB):
                token_major_out(3 * NB + b, dz1_tok, b)

            def rsig1_out(b):
                if b == 0:
                    act.wait_ge(bn_ready, 1)
                    act.wait_ge(dz1_done, NB)
                sigmoid(b, rz1_mm, b + 1, bank[RZ1[b]], r_sig1, bn[:, 0:1], rsig1_ready)

            def rsig2_out(b):
                sigmoid(b, rz2_mm, b + 1, bank[RZ2[b]], r_sig2, bn[:, 1:2], rsig2_ready)

            def zT_out(b):
                act.wait_ge(zt_tr, b + 1)
                copy(cut(zT, b), bank[7][:], zT_ready, scale=col(G), bias=col(BB))
                copy(cut(z_hi, b), bank[7][:], zhi_done, scale=col(G), bias=col(BB))

            def exponentials(b):
                act.wait_ge(lg_shift, b + 1)
                act.activation(tok(ex, b), tok(lg, b), ACT.Exp).then_inc(ex_ready, 1)

            def wT_out(b):
                act.wait_ge(w_tr, b + 1)
                copy(cut(wT, b), bank[5][:], wT_ready)

            rsig1_out(0)
            rsig1_out(1)
            rsig2_out(0)
            rsig1_out(2)
            rsig2_out(1)
            rsig1_out(3)
            rsig2_out(2)
            rsig2_out(3)
            zT_out(0)
            exponentials(0)

            def gelu(n):
                act.wait_ge(h_mm, n + 1)
                if n >= RING:
                    act.wait_ge(t_done, n - RING + 1)
                act.activation(g_buf[n % RING], bank[n % 2][:], ACT.Gelu,
                               bias=col(FB1 + n % UB)).then_inc(g_done, 1)

            def hi(n):
                act.wait_ge(t_done, n + 1)
                if n >= SPLIT_RING:
                    act.wait_ge(y_mm, n - SPLIT_RING + 1)
                copy(hi_buf[n % SPLIT_RING][:], t_buf[n % RING], hi_done)

            for n in range(4):
                gelu(n)
            wT_out(0)
            hi(0)
            zT_out(1)
            hi(1)
            gelu(4)
            hi(2)
            for j in range(NB):
                for i in range(UB):
                    n = j * UB + i
                    if n + H_AHEAD < UNITS:
                        gelu(n + H_AHEAD)
                    if n + HI_AHEAD < UNITS:
                        hi(n + HI_AHEAD)
                    if i == EXP and j + 1 < NB:
                        exponentials(j + 1)
                    if i == Z_TR and j + 2 < NB:
                        zT_out(j + 2)
                    if i == W_TR and j + 1 < NB:
                        wT_out(j + 1)
                act.wait_ge(y_mm, (j + 1) * UB)
                act.activation(cut(oT, j), bank[6][:], ACT.Identity).then_inc(oT_ready, 1)

        @block.vector
        def _(dve):
            steps = [0]

            def link(ins):
                steps[0] += 1
                count = steps[0]
                ins.then_inc(dve_step, 1)
                yield
                dve.wait_ge(dve_step, count)

            def run(*pieces):
                pieces = list(pieces)
                while pieces:
                    pieces = [p for p in pieces if next(p, "end") != "end"]

            def advance(pieces, count):
                for _ in range(count):
                    next(pieces, None)

            def span(b):
                return slice(TB * b, TB * b + TB)

            def statistics(ln, b, source):
                for i, t in enumerate(tiles(b)):
                    last = dve.bn_stats(stats[:, t, :], source(i, t))
                yield from link(last)
                for t in tiles(b):
                    last = dve.bn_aggr(mv[:, ln, t, :], stats[:, t, :])
                yield from link(last)

            def plus_eps(ln, b):
                dve.tensor_scalar(vpe[:, ln, span(b)], mv[:, ln, span(b), 1], LN_EPS, None,
                                  ALU.add).then_inc(vpe_ready[ln], 1)

            def normalise(ln, b, into, source, scale):
                for t in tiles(b):
                    last = dve.tensor_scalar(into[:, t, :], source[:, t, :], mv[:, ln, t, 0:1],
                                             scale[:, t:t + 1], ALU.subtract, ALU.mult)
                return last

            def x_stats(b):
                dve.wait_ge(x_in[b], 16)
                run(statistics(LX, b, lambda i, t: x_tok[:, t, :]))
                plus_eps(LX, b)

            def x_norm(b):
                dve.wait_ge(rstd_ready[LX], b + 1)
                normalise(LX, b, xn_tok, x_tok, rstd[:, LX, :]).then_inc(xn_ready, 1)

            def layer1(b):
                dve.wait_ge(sig1_ready, b + 1)
                dve.scalar_tensor_tensor(out=cut(s1, b), in0=bank[4 + b % 2][:], scalar=col(B1),
                                         in1=cut(sig1, b), op0=ALU.add, op1=ALU.mult).then_inc(s1_done, 1)
                dve.wait_ge(s1_done, b + 1)
                dve.tensor_tensor(cut(h1T, b), cut(s1, b), cut(kT, b), ALU.add).then_inc(h1_done, 1)

            def layer2(b):
                dve.wait_ge(sig2_ready, b + 1)
                dve.scalar_tensor_tensor(out=cut(s2, b), in0=bank[b % 2][:], scalar=col(B2),
                                         in1=cut(sig2, b), op0=ALU.add, op1=ALU.mult).then_inc(s2_done, 1)
                dve.wait_ge(s2_done, b + 1)
                dve.wait_ge(hv_done, b + 1)
                dve.tensor_tensor(cut(hvT, b), cut(s2, b), cut(hvT, b), ALU.add).then_inc(e_done, 1)
                dve.scalar_tensor_tensor(out=cut(u2T, b), in0=cut(s2, b), scalar=1.0, in1=cut(sig2, b),
                                         op0=ALU.subtract, op1=ALU.mult).then_inc(u2_done, 1)
                dve.wait_ge(e_done, b + 1)
                dve.scalar_tensor_tensor(out=cut(dpT, b), in0=cut(hvT, b), scalar=GRAD_SCALE,
                                         in1=cut(alrT, b), op0=ALU.mult, op1=ALU.mult).then_inc(dp_done, 1)
                dve.scalar_tensor_tensor(out=cut(u1T, b), in0=cut(s1, b), scalar=1.0, in1=cut(sig1, b),
                                         op0=ALU.subtract, op1=ALU.mult).then_inc(u1_done, 1)
                dve.wait_ge(dp_done, b + 1)
                dve.wait_ge(d2_done, b + 1)
                dve.scalar_tensor_tensor(out=cut(dz2T, b), in0=cut(dpT, b), scalar=1.0, in1=cut(d2T, b),
                                         op0=ALU.mult, op1=ALU.mult,
                                         accum_out=gb[:, 1, b:b + 1]).then_inc(dz2_done, 1)

            def layer1_back(b):
                dve.wait_ge(dh1_mm, b + 1)
                dve.tensor_tensor(cut(dh1T, b), bank[6 + b % 2][:], cut(dpT, b), ALU.add).then_inc(dh1_done, 1)
                dve.wait_ge(dh1_done, b + 1)
                dve.wait_ge(d1_done, b + 1)
                dve.scalar_tensor_tensor(out=cut(dz1T, b), in0=cut(dh1T, b), scalar=1.0, in1=cut(d1T, b),
                                         op0=ALU.mult, op1=ALU.mult,
                                         accum_out=gb[:, 0, b:b + 1]).then_inc(dz1_done, 1)

            def adam(new, old, g, tmp, rcp, ready):
                yield from link(dve.tensor_scalar(tmp, g, -1.0, ADAM_EPS, ALU.mult, ALU.add))
                yield from link(dve.scalar_tensor_tensor(out=tmp, in0=g, scalar=ADAM_EPS, in1=tmp, op0=ALU.add,
                                              op1=ALU.max))
                yield from link(dve.reciprocal(rcp, tmp))
                yield from link(dve.scalar_tensor_tensor(out=tmp, in0=g, scalar=-LR, in1=rcp, op0=ALU.mult, op1=ALU.mult))
                last = dve.scalar_tensor_tensor(out=new, in0=old, scalar=1.0 - LR * WD, in1=tmp,
                                                op0=ALU.mult, op1=ALU.add)
                last.then_inc(ready, 1)

            dve.memset(b2_stack[:], 0.0).then_inc(b2_zero, 1)
            x_stats(0)
            x_stats(1)
            x_norm(0)
            x_stats(2)
            x_norm(1)
            x_stats(3)
            x_norm(2)
            dve.wait_ge(cols_ready, 1)
            layer1(0)
            x_norm(3)
            for b in range(1, NB):
                layer1(b)
            for b in range(NB):
                layer2(b)
                if b:
                    layer1_back(b - 1)
            layer1_back(NB - 1)
            dve.wait_ge(gw2_mm, 1)
            run(adam(w2n[:], w2_sb[:], bank[5][:, 0:P], adam_tmp[:, 0, :], adam_tmp[:, 1, :], w2n_ready))
            dve.wait_ge(dz1_done, NB)
            run(link(dve.tensor_reduce(gbs[:], gb[:], AX_X, ALU.add)))
            run(adam(bn[:], cols[:, B1:B1 + 2], gbs[:], gb_tmp[:], gb[:, 0, 0:2], bn_ready))
            dve.wait_ge(w2n_ready, 1)
            dve.wait_ge(gw1_mm, 1)
            run(adam(w1n[:], w1_sb[:], bank[1][:, 0:P], adam_tmp[:, 0, :], adam_tmp[:, 1, :], w1n_ready))
            dve.wait_ge(bn_ready, 1)

            def retrieve1(b):
                dve.wait_ge(rsig1_ready, b + 1)
                dve.scalar_tensor_tensor(out=cut(r_sig1, b), in0=bank[RZ1[b]][:], scalar=bn[:, 0:1],
                                         in1=cut(r_sig1, b), op0=ALU.add, op1=ALU.mult).then_inc(rs1_done, 1)
                dve.wait_ge(rs1_done, b + 1)
                dve.wait_ge(qT_ready, b + 1)
                dve.tensor_tensor(cut(r_h1T, b), cut(r_sig1, b), cut(qT, b), ALU.add).then_inc(rh1_done, 1)

            def retrieve2(b):
                dve.wait_ge(rsig2_ready, b + 1)
                dve.scalar_tensor_tensor(out=cut(r_sig2, b), in0=bank[RZ2[b]][:], scalar=bn[:, 1:2],
                                         in1=cut(r_sig2, b), op0=ALU.add, op1=ALU.mult).then_inc(rs2_done, 1)
                dve.wait_ge(rs2_done, b + 1)
                dve.tensor_tensor(cut(rT, b), cut(r_sig2, b), cut(r_h1T, b), ALU.add).then_inc(r_done, 1)

            def norm_r(b):
                dve.wait_ge(r_tr, b + 1)
                yield from statistics(LR_, b, lambda i, t: bank[4][:, i * P:(i + 1) * P])
                plus_eps(LR_, b)

            def residual(b):
                dve.wait_ge(rstd_ready[LR_], b + 1)
                for i, t in enumerate(tiles(b)):
                    last = dve.scalar_tensor_tensor(out=x1_tok[:, t, :], in0=bank[4][:, i * P:(i + 1) * P],
                                                    scalar=rstd[:, LR_, t:t + 1], in1=x_tok[:, t, :],
                                                    op0=ALU.mult, op1=ALU.add)
                last.then_inc(x1_ready, 1)
                dve.tensor_tensor(shift[:, 0, span(b)], mv[:, LR_, span(b), 0], rstd[:, LR_, span(b)],
                                  ALU.mult).then_inc(shift_ready, 1)
                yield
                dve.wait_ge(x1_ready, b + 1)
                yield from statistics(L1, b, lambda i, t: x1_tok[:, t, :])
                dve.tensor_scalar(vpe[:, LZ, span(b)], mv[:, L1, span(b), 1], 1.0 + LN_EPS, LN_EPS * LN_EPS,
                                  ALU.mult, ALU.add).then_inc(vpe_ready[LZ], 1)
                plus_eps(L1, b)

            def norm_z(b):
                dve.wait_ge(rstd_ready[LZ], b + 1)
                normalise(L1, b, zt_tok, x1_tok, rstd[:, LZ, :]).then_inc(zt_ready, 1)

            def z_low(b):
                dve.wait_ge(zhi_done, b + 1)
                dve.tensor_tensor(cut(z_lo, b), cut(zT, b), cut(z_hi, b).bitcast(F32),
                                  ALU.subtract).then_inc(zlo_done, 1)

            def norms(b):
                yield from norm_r(b)
                yield
                yield from residual(b)
                yield
                norm_z(b)

            def wide(v):
                return v.unsqueeze(2).to_broadcast([P, TB, E])

            def small(i, b):
                return red[:, i, span(b)]

            MX, SM, RS, M1, F1, M2, F2, DN = range(8)

            def first_largest(b, source, most, rank, onehot):
                yield from link(dve.tensor_reduce(small(most, b), source, AX_X, ALU.max))
                yield from link(dve.tensor_tensor(tok(eq, b), source, wide(small(most, b)), ALU.is_equal))
                yield from link(dve.tensor_tensor(tok(eq, b), tok(eq, b), ramp[:], ALU.mult))
                yield from link(dve.tensor_reduce(small(rank, b), tok(eq, b), AX_X, ALU.max))
                yield from link(dve.tensor_tensor(tok(onehot, b), tok(eq, b), wide(small(rank, b)),
                                                  ALU.is_equal))

            def router(b):
                if b == 0:
                    dve.wait_ge(rb_in, 16)
                    dve.wait_ge(ramp_ready, 1)
                dve.wait_ge(lg_mm, b + 1)
                dve.tensor_tensor(tok(lg, b), bank[4][:, 0:TB * E].rearrange("p (t e) -> p t e", e=E),
                                  rb_b[:].unsqueeze(1).to_broadcast([P, TB, E]), ALU.add).then_inc(lg_read, 1)
                yield
                dve.wait_ge(lg_read, b + 1)
                yield from link(dve.tensor_reduce(small(MX, b), tok(lg, b), AX_X, ALU.max))
                dve.tensor_tensor(tok(lg, b), tok(lg, b), wide(small(MX, b)),
                                  ALU.subtract).then_inc(lg_shift, 1)
                for _ in range(EXP_PIECES):
                    yield
                dve.wait_ge(ex_ready, b + 1)
                yield from link(dve.tensor_reduce(small(SM, b), tok(ex, b), AX_X, ALU.add))
                yield from link(dve.reciprocal(small(RS, b), small(SM, b)))
                yield from link(dve.tensor_tensor(tok(pr, b), tok(ex, b), wide(small(RS, b)), ALU.mult))
                yield from first_largest(b, tok(pr, b), M1, F1, oh1)
                yield from link(dve.scalar_tensor_tensor(out=tok(ex, b), in0=tok(oh1, b), scalar=-2.0,
                                                         in1=tok(pr, b), op0=ALU.mult, op1=ALU.add))
                yield from first_largest(b, tok(ex, b), M2, F2, oh2)
                dve.tensor_tensor(tok(oh1, b), tok(oh1, b), tok(oh2, b), ALU.add)
                yield from link(dve.tensor_tensor(small(DN, b), small(M1, b), small(M2, b), ALU.add))
                dve.tensor_tensor(tok(oh1, b), tok(oh1, b), tok(pr, b), ALU.mult)
                yield from link(dve.tensor_scalar(small(DN, b), small(DN, b), 1e-8, None, ALU.max))
                yield from link(dve.reciprocal(small(RS, b), small(DN, b)))
                yield from link(dve.tensor_tensor(tok(pr, b), tok(oh1, b), wide(small(RS, b)), ALU.mult))
                yield from link(dve.tensor_copy(tok(w_hi, b), tok(pr, b)))
                dve.wait_ge(wpad_zero, b + 1)
                dve.tensor_copy(w_pad[:, TB * b:TB * b + TB, 0:E], tok(w_hi, b).bitcast(F32))
                dve.tensor_tensor(w_pad[:, TB * b:TB * b + TB, E:2 * E], tok(pr, b),
                                  tok(w_hi, b).bitcast(F32), ALU.subtract).then_inc(w_ready, 1)

            def weigh(n):
                dve.wait_ge(g_done, n + 1)
                if n % C == 0:
                    dve.wait_ge(wb_mm, n // C + 1)
                if n >= RING:
                    dve.wait_ge(lo_done, n - RING + 1)
                dve.tensor_tensor(t_buf[n % RING], g_buf[n % RING], bank[2 + n // C % 2][:],
                                  ALU.mult).then_inc(t_done, 1)

            def y_stats(b):
                dve.wait_ge(o_tr, b + 1)
                dve.wait_ge(rstd_ready[L1], b + 1)
                for i, t in enumerate(tiles(b)):
                    last = dve.scalar_tensor_tensor(out=y_tok[:, t, :], in0=x1_tok[:, t, :],
                                                    scalar=rstd[:, L1, t:t + 1],
                                                    in1=bank[5][:, i * P:(i + 1) * P],
                                                    op0=ALU.mult, op1=ALU.add)
                last.then_inc(y_ready, 1)
                yield
                dve.wait_ge(y_ready, b + 1)
                yield from statistics(LY, b, lambda i, t: y_tok[:, t, :])
                plus_eps(LY, b)

            def y_norm(b):
                dve.wait_ge(rstd_ready[LY], b + 1)
                dve.wait_ge(shift_ready, b + 1)
                yield from link(dve.scalar_tensor_tensor(out=shift[:, 1, span(b)], in0=mv[:, LY, span(b), 0],
                                                         scalar=-1.0, in1=rstd[:, LY, span(b)],
                                                         op0=ALU.mult, op1=ALU.mult))
                yield from link(dve.tensor_tensor(shift[:, 1, span(b)], shift[:, 1, span(b)],
                                                  shift[:, 0, span(b)], ALU.subtract))
                for t in tiles(b):
                    last = dve.tensor_scalar(y_tok[:, t, :], y_tok[:, t, :], rstd[:, LY, t:t + 1],
                                             shift[:, 1, t:t + 1], ALU.mult, ALU.add)
                yield from link(last)
                dve.tensor_tensor(tok(x1_tok, b), tok(x1_tok, b), tok(y_tok, b), ALU.add).then_inc(yn_done, 1)

            retrieve1(0)
            retrieve1(1)
            retrieve2(0)
            retrieve1(2)
            run(norm_r(0))
            retrieve1(3)
            run(residual(0))
            retrieve2(1)
            norm_z(0)
            retrieve2(2)
            retrieve2(3)
            z_low(0)
            run(router(0), norms(1))
            for n in range(T_AHEAD):
                weigh(n)
                if n == 1:
                    z_low(1)
            for j in range(NB):
                result_stats, result = y_stats(j - 1), y_norm(j - 1)
                routing = router(j + 1)
                r_stats, x1 = norm_r(j + 2), residual(j + 2)
                for i in range(UB):
                    n = j * UB + i
                    if n + T_AHEAD < UNITS:
                        weigh(n + T_AHEAD)
                    if j:
                        if i >= Y_STATS:
                            advance(result_stats, 2)
                        if i >= Y_NORM:
                            advance(result, 2)
                    if j + 1 < NB and i >= ROUTER:
                        advance(routing, ROUTER_STEPS if i < W_TR - 1 else UB * UB)
                    if j + 2 < NB:
                        if i >= NORM_R:
                            advance(r_stats, 2)
                        if i >= RESIDUAL:
                            advance(x1, 2)
                        if i == NORM_Z:
                            norm_z(j + 2)
                        if i == Z_LOW:
                            z_low(j + 2)
            run(y_stats(NB - 1))
            run(y_norm(NB - 1))


_INS = ['L0_attn_x', 'L0_attn_Wk', 'L0_attn_bk', 'L0_attn_Wq', 'L0_attn_bq', 'L0_attn_Wv', 'L0_attn_bv',
        'L0_attn_Wlr', 'L0_attn_blr', 'L0_attn_W1', 'L0_attn_b1', 'L0_attn_W2', 'L0_attn_b2',
        'L0_ffn_ln_g', 'L0_ffn_ln_b', 'L0_ffn_rW', 'L0_ffn_rb', 'L0_ffn_W1', 'L0_ffn_b1', 'L0_ffn_W2',
        'L0_ffn_b2']
_OUTS = [((8, 256, 128), 'float32')]


def kernel(**inputs):
    import numpy as _np
    import concourse.bacc as _bacc
    from concourse import mybir as _mybir
    from concourse.bass_utils import run_bass_kernel_spmd as _run

    nc = _bacc.Bacc("TRN2", target_bir_lowering=False, num_devices=1)
    arrays, args = {}, []
    for name in _INS:
        a = _np.ascontiguousarray(inputs[name])
        arrays[f"in_{name}_dram"] = a
        args.append(nc.dram_tensor(f"in_{name}_dram", a.shape, _mybir.dt.from_np(a.dtype), kind="ExternalInput").ap())
    for i, (shape, dtype) in enumerate(_OUTS):
        dt = _mybir.dt.from_np(_np.dtype(dtype))
        args.append(nc.dram_tensor(f"out_{i}_dram", shape, dt, kind="ExternalOutput").ap())
    memory_and_experts(nc, *args)
    r = _run(nc, [arrays], core_ids=[0])
    return r.results[0]["out_0_dram"]
```

```python
from contextlib import ExitStack

import concourse.bass as bass
from concourse import mybir

ALU = mybir.AluOpType
ACT = mybir.ActivationFunctionType
AX_X = mybir.AxisListType.X
F32 = mybir.dt.float32
F32R = mybir.dt.float32r
ENG = mybir.EngineType

P = 128
BLOCK = 512
LN_EPS = 1e-5
LR = 0.01
WD = 0.01
MAX_ALR = 0.1
ADAM_EPS = 1e-8


def widths(D, E, HF):
    packs = []
    for names in ((("Wk", D), ("Wv", D), ("W1", D), ("Wlr", D), ("blr", 1), ("vectors", 7 + E * HF // D)),
                  (("W2", D), ("W2T", D), ("Wq", D), ("rW", E), ("rb", E), ("b2", D))):
        pack, first = {}, 0
        for name, width in names:
            pack[name] = (first, width)
            first += width
        packs.append((pack, first))
    return packs


def memory_and_experts(nc, x, early, late, fW1, fW2, out):
    B, S, D = x.shape
    E, H, HF = fW1.shape
    N = B * S
    T = N // P
    NB = N // BLOCK
    TB = BLOCK // P
    C = HF // P
    assert D == P and H == P and T == NB * TB
    UNITS = NB * E * C
    UB = E * C
    THIRD = 32
    PIECES = 4
    GRAD_SCALE = 2.0 * MAX_ALR / D

    x_v = x.rearrange("b s d -> (b s) d").rearrange("(p t) d -> p t d", p=P)
    out_v = out.rearrange("b s d -> (b s) d").rearrange("(p t) d -> p t d", p=P)

    with ExitStack() as ctx:
        def sb(name, shape, dt=F32):
            return ctx.enter_context(nc.sbuf_tensor(name, shape, dt))

        def sem(name):
            return ctx.enter_context(nc.semaphore(name))

        bank = [ctx.enter_context(nc.psum_tensor(f"bank{i}", [P, BLOCK], F32)) for i in range(8)]

        x_tok = sb("x_tok", [P, T, D])
        xn_tok = sb("xn_tok", [P, T, D])
        x1_tok = xn_tok
        xnT = sb("xnT", [P, N])
        kT = sb("kT", [P, N])
        vT = sb("vT", [P, N])
        sig1 = sb("sig1", [P, N])
        s1 = sb("s1", [P, N])
        h1T = sb("h1T", [P, N])
        sig2 = sb("sig2", [P, N])
        s2 = sb("s2", [P, N])
        alrT = sb("alrT", [P, N])
        qT = sb("qT", [P, N])
        k_tok = sb("k_tok", [P, T, D])
        h1_tok = sb("h1_tok", [P, T, D])
        dz2_tok = kT[:].rearrange("p (t d) -> p t d", d=D)
        dz1_tok = h1T[:].rearrange("p (t d) -> p t d", d=D)
        hvT, dh1T = vT, vT
        dpT = alrT
        u2T, dz2T = sig2, sig2
        d2T = sig2
        u1T, dz1T = sig1, sig1
        d1T = s1
        r_sig1, r_h1T, r_sig2, rT = s1, xnT, s2, vT
        zT = alrT
        zt_tok = h1_tok
        w_pad = qT[:].rearrange("p (t d) -> p t d", d=P)
        z_hi = sb("z_hi", [P, N], F32R)
        z_lo = sb("z_lo", [P, N], F32R)
        wT = sb("wT", [P, N], F32R)
        fW_raw = sb("fW_raw", [P, E * HF])
        fW1_hi = sb("fW1_hi", [P, E * HF], F32R)
        fW1_lo = sb("fW1_lo", [P, E * HF], F32R)
        fW2_hi = sb("fW2_hi", [P, E * C * H], F32R)
        fW2_lo = sb("fW2_lo", [P, E * C * H], F32R)
        sel = sb("sel", [P, E], F32R)
        def buffers(*tensors):
            return [tensor[:, i * BLOCK:(i + 1) * BLOCK] for tensor in tensors for i in range(NB)]

        g_buf = buffers(sig1, h1T, k_tok[:].rearrange("p t d -> p (t d)"))
        t_buf = buffers(s1, sig2)
        G_RING, T_RING, SPLIT_RING = len(g_buf), len(t_buf), 5
        oT = s2
        y_tok = xnT[:].rearrange("p (t d) -> p t d", d=D)
        hi_buf = [sb(f"hi_buf{i}", [P, BLOCK], F32R) for i in range(SPLIT_RING)]
        lo_buf = [sb(f"lo_buf{i}", [P, BLOCK], F32R) for i in range(SPLIT_RING)]

        ident = sb("ident", [P, P])
        (early_at, early_width), (late_at, late_width) = widths(D, E, HF)
        early_sb = sb("early_sb", [P, early_width])
        late_sb = sb("late_sb", [P, late_width])

        def part(pack, at, name):
            first, width = at[name]
            return pack[:, first:first + width]

        wk_sb, wv_sb, w1_sb, wlr_b, blr_b, cols = (part(early_sb, early_at, n) for n in early_at)
        w2_sb, w2T_sb, wq_sb, rw_sb, rb_b, b2_stack = (part(late_sb, late_at, n) for n in late_at)
        BK, BQ, BV, B1, B2, G, BB, FB1 = range(8)
        w1n, w2n = sb("w1n", [P, P]), sb("w2n", [P, P])
        adam_tmp = sb("adam_tmp", [P, 2, P])
        gb = sb("gb", [P, 2, NB])
        gbs = sb("gbs", [P, 2])
        gb_tmp = sb("gb_tmp", [P, 2])
        bn = sb("bn", [P, 2])
        b2_parts = sb("b2_parts", [P, H], F32R)
        stats = sb("stats", [P, T, 6])
        LX, LR_, L1, LZ, LY = range(5)
        mv = sb("mv", [P, 5, T, 2])
        vpe = sb("vpe", [P, 5, T])
        rstd = sb("rstd", [P, 5, T])
        shift = sb("shift", [P, 2, T])
        minus_half = sb("minus_half", [P, TB])
        ramp = sb("ramp", [P, TB, E])
        lg, ex, pr, eq, oh1, oh2 = (kT[:, i * T * E:(i + 1) * T * E].rearrange("p (t e) -> p t e", e=E)
                                    for i in range(6))
        w_hi = sb("w_hi", [P, T, E], F32R)
        red = kT[:, 6 * T * E:7 * T * E].rearrange("p (i t) -> p i t", t=T)

        x_in = [sem(f"x_in{i}") for i in range(NB)]
        early_in, late_in, fw1_in, fw2_in = (sem(n) for n in ("early_in", "late_in", "fw1_in", "fw2_in"))
        out_done = sem("out_done")
        zeroed, ident_ready, half_ready, table_ready, ramp_ready, wpad_zero = (sem(n) for n in (
            "zeroed", "ident_ready", "half_ready", "table_ready", "ramp_ready", "wpad_zero"))
        sel_ready, fw_hi_done, fw_lo_done, b2hi_done, b2lo_done = (sem(n) for n in (
            "sel_ready", "fw_hi_done", "fw_lo_done", "b2hi_done", "b2lo_done"))
        dve_step = sem("dve_step")
        vpe_ready = [sem(f"vpe_ready{i}") for i in range(5)]
        rstd_ready = [sem(f"rstd_ready{i}") for i in range(5)]
        xn_ready, k_mm, kT_ready, v_mm, vT_ready, z1_mm, sig1_ready = (sem(n) for n in (
            "xn_ready", "k_mm", "kT_ready", "v_mm", "vT_ready", "z1_mm", "sig1_ready"))
        s1_done, h1_done, hv_done, alr_mm, alr_ready, z2_mm, sig2_ready, s2_done = (sem(n) for n in (
            "s1_done", "h1_done", "hv_done", "alr_mm", "alr_ready", "z2_mm", "sig2_ready", "s2_done"))
        e_done, u2_done, d2_done, dz2_done, dh1_mm, dh1_done, u1_done, d1_done, dz1_done = (
            sem(n) for n in ("e_done", "u2_done", "d2_done", "dz2_done", "dh1_mm", "dh1_done",
                             "u1_done", "d1_done", "dz1_done"))
        tr_mm, tr_out, q_mm, qT_ready, gw2_mm, gw1_mm, w2n_ready, w1n_ready, bn_ready = (
            sem(n) for n in ("tr_mm", "tr_out", "q_mm", "qT_ready", "gw2_mm", "gw1_mm",
                             "w2n_ready", "w1n_ready", "bn_ready"))
        rz1_mm, rsig1_ready, rh1_done, rz2_mm, rsig2_ready, r_done, r_tr = (sem(n) for n in (
            "rz1_mm", "rsig1_ready", "rh1_done", "rz2_mm", "rsig2_ready", "r_done", "r_tr"))
        x1_ready, zt_ready, zt_tr, zT_ready, zhi_done, zlo_done = (
            sem(n) for n in ("x1_ready", "zt_ready", "zt_tr",
                             "zT_ready", "zhi_done", "zlo_done"))
        lg_mm, lg_shift, ex_ready, w_ready, w_tr, wT_ready = (sem(n) for n in (
            "lg_mm", "lg_shift", "ex_ready", "w_ready", "w_tr", "wT_ready"))
        rs1_done, rs2_done, shift_ready, lg_read, dp_done = (sem(n) for n in (
            "rs1_done", "rs2_done", "shift_ready", "lg_read", "dp_done"))
        h_mm, g_done, wb_mm, t_done, hi_done, lo_done, y_mm = (sem(n) for n in (
            "h_mm", "g_done", "wb_mm", "t_done", "hi_done", "lo_done", "y_mm"))
        lo_dve_done, oT_ready, o_tr, y_ready, yn_done = (sem(n) for n in (
            "lo_dve_done", "oT_ready", "o_tr", "y_ready", "yn_done"))

        TURNS = [("x", 0), ("x", 1), ("x", 2)]
        for w in range(NB + 1):
            TURNS += [turn for turn in (("dz2", w - 1), ("k", w), ("h1", w), ("dz1", w - 1), ("x", w + 3))
                      if 0 <= turn[1] < NB]

        PARTS = [(TB * b, TB) for b in range(NB - 1)] + [(T - TB, TB // 2), (T - TB // 2, TB // 2)]
        O_BANK = [5] * NB + [4]

        def part_tiles(q):
            return slice(PARTS[q][0], sum(PARTS[q]))

        def turn(kind, b):
            return TURNS.index((kind, b))

        WARM_UP = 22
        KEEP = (6, 10, 8, 34, 2, 2, 0, 6)

        Y_TR, Y_STATS, Y_NORM = 0, 1, 5
        ROUTER, EXP, ROUTE, ROUTE_STEPS, W_TR = (3, 0, 0), (3, 0, 0), (5, 2, 3), (5, 2, 3), 10
        R_TR, NORM_R, LR_POW, RESIDUAL, LZ_POW, NORM_Z, Z_TR, LOGITS, Z_LOW = 3, 4, 7, 10, 11, 13, 14, 15, 16

        def due(position, j, i):
            b, rest = divmod((j + 2) * UB + i - position, UB)
            return b if rest == 0 and 2 <= b < NB else None

        RZ1, RZ2 = (0, 1, 2, 0), (3, 5, 6, 2)

        LO_ON_DVE = range(UNITS - 7, UNITS, 2)

        H_AHEAD, WB_AHEAD, T_AHEAD, HI_AHEAD, LO_AHEAD = 10, 5, 4, 4, 3

        def tiles(b):
            return range(TB * b, TB * b + TB)

        def cut(tensor, b):
            return tensor[:, b * BLOCK:(b + 1) * BLOCK]

        def tok(tensor, b):
            return tensor[:, TB * b:TB * b + TB, :]

        def col(i):
            return cols[:, i:i + 1]

        def bank3(i):
            return bank[i][:].rearrange("p (t d) -> p t d", d=P)

        block = ctx.enter_context(nc.Block())

        @block.sync
        def _(sp):
            def load_x(b):
                sp.dma_start(tok(x_tok, b), tok(x_v, b)).then_inc(x_in[b], 16)

            load_x(0)
            sp.dma_start(early_sb[:], early).then_inc(early_in, 16)
            load_x(1)
            load_x(2)
            sp.dma_start(late_sb[:], late).then_inc(late_in, 16)
            load_x(3)
            sp.dma_start(fW_raw[:].rearrange("p (e f) -> p e f", f=HF),
                         fW1.rearrange("e h f -> h e f")).then_inc(fw1_in, 16)
            sp.wait_ge(fw_lo_done, PIECES)
            sp.dma_start(fW_raw[:].rearrange("p (e h) -> p e h", h=H),
                         fW2.rearrange("e (c f) h -> f (e c) h", f=P)).then_inc(fw2_in, 16)
            for q in range(len(PARTS)):
                sp.wait_ge(yn_done, q + 1)
                sp.dma_start(out_v[:, part_tiles(q), :], x1_tok[:, part_tiles(q), :]).then_inc(out_done, 16)
            sp.wait_ge(out_done, 16 * len(PARTS))

        @block.gpsimd
        def _(pool):
            pool.memset(ident[:], 0.0).then_inc(zeroed, 1)
            pool.wait_ge(zeroed, 1)
            pool.affine_select(out=ident[:], in_=ident[:], compare_op=ALU.not_equal, fill=1.0, base=0,
                               pattern=[[-1, P]], channel_multiplier=1).then_inc(ident_ready, 1)
            pool.memset(minus_half[:], -0.5).then_inc(half_ready, 1)
            pool.wait_ge(half_ready, 1)

            def rsqrt(ln, b, where=None):
                where = where or slice(TB * b, TB * b + TB)
                pool.wait_ge(vpe_ready[ln], b + 1)
                pool.tensor_tensor(rstd[:, ln, where], vpe[:, ln, where],
                                   minus_half[:, 0:where.stop - where.start],
                                   ALU.pow).then_inc(rstd_ready[ln], 1)

            rsqrt(LX, 0)
            rsqrt(LX, 1)
            rsqrt(LX, 2)
            rsqrt(LX, 3)
            pool.iota(ramp[:], pattern=[[0, TB], [-1, E]], base=E, channel_multiplier=0,
                      allow_small_or_imprecise_dtypes=True).then_inc(ramp_ready, 1)

            def split_weights(layer, piece, loaded, hi, lo):
                if piece == 0:
                    pool.wait_ge(loaded, 16)
                s = slice(piece * E * HF // PIECES, (piece + 1) * E * HF // PIECES)
                pool.tensor_scalar(hi[:, s], fW_raw[:, s], 1.0, 0.0, ALU.mult, ALU.add).then_inc(fw_hi_done, 1)
                pool.wait_ge(fw_hi_done, layer * PIECES + piece + 1)
                pool.tensor_tensor(lo[:, s], fW_raw[:, s], hi[:, s].bitcast(F32),
                                   ALU.subtract).then_inc(fw_lo_done, 1)

            pieces = [(0, piece, fw1_in, fW1_hi, fW1_lo) for piece in range(PIECES)]
            pieces += [(1, piece, fw2_in, fW2_hi, fW2_lo) for piece in range(PIECES)]
            split_weights(*pieces[0])
            for w in range(NB):
                pool.wait_ge(h1_done, w + 1)
                pool.wait_ge(vT_ready, w + 1)
                pool.tensor_tensor(cut(hvT, w), cut(h1T, w), cut(vT, w), ALU.subtract).then_inc(hv_done, 1)
                split_weights(*pieces[w + 1])
                pool.wait_ge(u2_done, w + 1)
                pool.tensor_tensor(cut(d2T, w), cut(s2, w), cut(u2T, w), ALU.subtract).then_inc(d2_done, 1)
                pool.wait_ge(u1_done, w + 1)
                pool.tensor_tensor(cut(d1T, w), cut(s1, w), cut(u1T, w), ALU.subtract).then_inc(d1_done, 1)
            for piece in pieces[NB + 1:]:
                split_weights(*piece)
            pool.wait_ge(ident_ready, 1)
            pool.tensor_tensor(sel[:], ident[:, 0:E], ident[:, E:2 * E], ALU.add).then_inc(sel_ready, 1)
            pool.wait_ge(late_in, 16)
            pool.tensor_scalar(b2_parts[:], b2_stack, 1.0, 0.0, ALU.mult, ALU.add).then_inc(b2hi_done, 1)

            def clear_w(b):
                pool.wait_ge(rh1_done, b + 1)
                pool.memset(w_pad[:, TB * b:TB * b + TB, :], 0.0).then_inc(wpad_zero, 1)

            clear_w(0)
            clear_w(1)
            rsqrt(LR_, 0)
            clear_w(2)
            rsqrt(LZ, 0)
            rsqrt(L1, 0)
            clear_w(3)
            rsqrt(LR_, 1)

            def lo(n):
                if n in LO_ON_DVE:
                    return
                pool.wait_ge(hi_done, n + 1)
                pool.tensor_tensor(lo_buf[n % SPLIT_RING][:], t_buf[n % T_RING], hi_buf[n % SPLIT_RING][:].bitcast(F32),
                                   ALU.subtract).then_inc(lo_done, 1)

            lo(0)
            lo(1)
            rsqrt(LZ, 1)
            lo(2)
            rsqrt(L1, 1)
            for j in range(NB):
                for i in range(UB):
                    n = j * UB + i
                    if n + LO_AHEAD < UNITS:
                        lo(n + LO_AHEAD)
                    if i == Y_STATS + 1 and j:
                        rsqrt(LY, j - 1)
                    if due(LR_POW, j, i):
                        rsqrt(LR_, due(LR_POW, j, i))
                    if due(LZ_POW, j, i):
                        rsqrt(LZ, due(LZ_POW, j, i))
                        rsqrt(L1, due(LZ_POW, j, i))
            for q in (NB - 1, NB):
                rsqrt(LY, q, part_tiles(q))

        @block.tensor
        def _(pe):
            def mm(out_, lhsT, rhs, start=True, stop=True):
                return pe.matmul(out_, lhsT, rhs, start=start, stop=stop)

            def transposed(kind, b, pieces):
                n = turn(kind, b)
                if n:
                    pe.wait_ge(tr_out, n)
                for i in range(TB):
                    last = pe.transpose(bank[7][:, i * P:(i + 1) * P], pieces(i), ident[:])
                last.then_inc(tr_mm, 1)

            def feature_major_x(b):
                pe.wait_ge(xn_ready, b + 1)
                transposed("x", b, lambda i: xn_tok[:, TB * b + i, :])

            def token_major(kind, source, b, ready):
                pe.wait_ge(ready, b + 1)
                transposed(kind, b, lambda i: source[:, b * BLOCK + i * P:b * BLOCK + (i + 1) * P])

            def k_product(b):
                pe.wait_ge(tr_out, turn("x", b) + 1)
                if b:
                    pe.wait_ge(kT_ready, b)
                mm(bank[1][:], wk_sb, cut(xnT, b)).then_inc(k_mm, 1)

            def q_product(b):
                pe.wait_ge(late_in, 16)
                if b:
                    pe.wait_ge(qT_ready, b)
                else:
                    pe.wait_ge(kT_ready, NB)
                mm(bank[1][:], wq_sb, cut(xnT, b)).then_inc(q_mm, 1)

            def v_product(b):
                if b:
                    pe.wait_ge(alr_ready, b)
                mm(bank[2][:], wv_sb, cut(xnT, b)).then_inc(v_mm, 1)

            def alr_product(b):
                pe.wait_ge(vT_ready, b + 1)
                mm(bank[2][:], wlr_b, cut(xnT, b)).then_inc(alr_mm, 1)

            def z1_product(b):
                pe.wait_ge(kT_ready, b + 1)
                if b:
                    pe.wait_ge(sig1_ready, b)
                    pe.wait_ge(s1_done, b)
                mm(bank[3][:], w1_sb, cut(kT, b)).then_inc(z1_mm, 1)

            def z2_product(b):
                pe.wait_ge(h1_done, b + 1)
                if b == 0:
                    pe.wait_ge(late_in, 16)
                else:
                    pe.wait_ge(sig2_ready, b)
                    pe.wait_ge(s2_done, b)
                mm(bank[5][:], w2_sb, cut(h1T, b)).then_inc(z2_mm, 1)

            def dh1_product(b):
                pe.wait_ge(dz2_done, b + 1)
                if b:
                    pe.wait_ge(dh1_done, b)
                mm(bank[6][:], w2T_sb, cut(dz2T, b)).then_inc(dh1_mm, 1)

            def gradient(into, left, right, b, kind, done):
                pe.wait_ge(tr_out, turn(kind, b) + 1)
                for t in tiles(b):
                    last = mm(into, left[:, t, :], right[:, t, :], start=(t == 0), stop=(t == T - 1))
                if b == NB - 1:
                    last.then_inc(done, 1)

            def keep_clock(scratch, count):
                for _ in range(count):
                    pe.transpose(bank[scratch][:, 0:P], ident[:], ident[:])

            pe.wait_ge(ident_ready, 1)
            keep_clock(6, WARM_UP)
            feature_major_x(0)
            pe.wait_ge(early_in, 16)
            k_product(0)
            feature_major_x(1)
            v_product(0)
            z1_product(0)
            k_product(1)
            alr_product(0)
            feature_major_x(2)
            for w in range(NB + 1):
                if w:
                    dh1_product(w - 1)
                    token_major("dz2", dz2T, w - 1, dz2_done)
                if w < NB:
                    z2_product(w)
                if w + 1 < NB:
                    v_product(w + 1)
                if w < NB:
                    token_major("k", kT, w, kT_ready)
                if w == NB:
                    q_product(1)
                if w:
                    gradient(bank[0][:, 0:P], h1_tok, dz2_tok, w - 1, "dz2", gw2_mm)
                if w + 1 < NB:
                    z1_product(w + 1)
                if w < NB:
                    token_major("h1", h1T, w, h1_done)
                if w + 1 < NB:
                    alr_product(w + 1)
                if w:
                    token_major("dz1", dz1T, w - 1, dz1_done)
                if w + 2 < NB:
                    k_product(w + 2)
                if w + 3 < NB:
                    feature_major_x(w + 3)
                if w >= NB - 1:
                    q_product(0 if w < NB else 2)
                if w:
                    gradient(bank[4][:, 0:P], k_tok, dz1_tok, w - 1, "dz1", gw1_mm)
            q_product(NB - 1)
            keep_clock(7, KEEP[0])

            def rz1_product(b):
                if b == 0:
                    pe.wait_ge(w1n_ready, 1)
                pe.wait_ge(qT_ready, NB)
                if b == NB - 1:
                    pe.wait_ge(rs1_done, 1)
                mm(bank[RZ1[b]][:], w1n[:], cut(qT, b)).then_inc(rz1_mm, 1)

            def rz2_product(b):
                pe.wait_ge(rh1_done, b + 1)
                if b == 0:
                    pe.wait_ge(w2n_ready, 1)
                    pe.wait_ge(dh1_done, NB)
                if b == NB - 1:
                    pe.wait_ge(rs1_done, 3)
                mm(bank[RZ2[b]][:], w2n[:], cut(r_h1T, b)).then_inc(rz2_mm, 1)

            def r_transpose(b):
                pe.wait_ge(r_done, b + 1)
                if b:
                    pe.wait_ge(lg_read, b)
                for i in range(TB):
                    last = pe.transpose(bank[4][:, i * P:(i + 1) * P],
                                        rT[:, b * BLOCK + i * P:b * BLOCK + (i + 1) * P], ident[:])
                last.then_inc(r_tr, 1)

            def z_transpose(b):
                pe.wait_ge(zt_ready, b + 1)
                if b:
                    pe.wait_ge(zhi_done, b)
                else:
                    pe.wait_ge(dh1_done, NB)
                for i, t in enumerate(tiles(b)):
                    last = pe.transpose(bank[7][:, i * P:(i + 1) * P], zt_tok[:, t, :], ident[:])
                last.then_inc(zt_tr, 1)

            def logits(b):
                pe.wait_ge(zT_ready, b + 1)
                pe.wait_ge(x1_ready, b + 1)
                for i, t in enumerate(tiles(b)):
                    last = mm(bank[4][:, i * E:(i + 1) * E], zT[:, t * P:(t + 1) * P], rw_sb)
                last.then_inc(lg_mm, 1)

            def w_transpose(b):
                pe.wait_ge(w_ready, b + 1)
                if b >= 2:
                    pe.wait_ge(y_ready, b - 1)
                elif b:
                    pe.wait_ge(wT_ready, b)
                for i, t in enumerate(tiles(b)):
                    last = pe.transpose(bank[5][:, i * P:(i + 1) * P], w_pad[:, t, :], ident[:])
                last.then_inc(w_tr, 1)

            rz1_product(0)
            rz1_product(1)
            keep_clock(7, KEEP[1])
            rz2_product(0)
            rz1_product(2)
            keep_clock(7, KEEP[2])
            r_transpose(0)
            rz1_product(3)
            rz2_product(1)
            rz2_product(2)
            keep_clock(7, KEEP[3])
            rz2_product(3)
            keep_clock(7, KEEP[4])
            z_transpose(0)
            pe.wait_ge(rs2_done, 3)
            keep_clock(6, 3)
            logits(0)

            def product3(into, w_hi, w_lo, a_hi, a_lo, start, stop):
                mm(into, w_hi, a_hi, start=start, stop=False)
                mm(into, w_lo, a_hi, start=False, stop=False)
                return mm(into, w_hi, a_lo, start=False, stop=stop)

            def weights(n):
                j, i = divmod(n, UB)
                e = i // C
                pe.wait_ge(wT_ready, j + 1)
                if n >= 2 * C:
                    pe.wait_ge(t_done, n - C)
                mm(bank[2 + e % 2][:], sel[:, e:e + 1].to_broadcast([P, P]), cut(wT, j)).then_inc(wb_mm, 1)

            def hidden(n):
                j, i = divmod(n, UB)
                s = slice(i * P, (i + 1) * P)
                if i == 0:
                    pe.wait_ge(zhi_done, j + 1)
                    pe.wait_ge(zlo_done, j + 1)
                if n >= 2:
                    pe.wait_ge(g_done, n - 1)
                product3(bank[n % 2][:], fW1_hi[:, s], fW1_lo[:, s], cut(z_hi, j), cut(z_lo, j),
                         True, True).then_inc(h_mm, 1)

            def output(n):
                i = n % UB
                s = slice(i * H, (i + 1) * H)
                if n in LO_ON_DVE:
                    pe.wait_ge(lo_dve_done, LO_ON_DVE.index(n) + 1)
                else:
                    pe.wait_ge(lo_done, n + 1 - sum(m < n for m in LO_ON_DVE))
                product3(bank[6][:], fW2_hi[:, s], fW2_lo[:, s], hi_buf[n % SPLIT_RING][:], lo_buf[n % SPLIT_RING][:],
                         False, i == UB - 1).then_inc(y_mm, 1)

            def bias_term(j):
                if j:
                    pe.wait_ge(oT_ready, j)
                mm(bank[6][:], b2_parts[:], cut(wT, j), start=True, stop=False)

            def final_transpose(q):
                pe.wait_ge(oT_ready, q + 1)
                pe.wait_ge(wT_ready, min(q + 2, NB))
                if q == NB - 1:
                    pe.wait_ge(y_ready, q)
                first, count = PARTS[q]
                for i in range(count):
                    last = pe.transpose(bank[O_BANK[q]][:, i * P:(i + 1) * P],
                                        oT[:, (first + i) * P:(first + i + 1) * P], ident[:])
                last.then_inc(o_tr, 1)

            pe.wait_ge(fw_lo_done, 2 * PIECES)
            pe.wait_ge(rs1_done, NB)
            hidden(0)
            r_transpose(1)
            hidden(1)
            keep_clock(6, KEEP[5])
            for n in (2, 3, 4, 5):
                hidden(n)
            w_transpose(0)
            hidden(6)
            hidden(7)
            pe.wait_ge(sel_ready, 1)
            pe.wait_ge(b2lo_done, 1)
            pe.wait_ge(rs2_done, NB)
            weights(0)
            bias_term(0)
            weights(C)
            hidden(8)
            weights(2 * C)
            hidden(9)
            for j in range(NB):
                for i in range(UB):
                    n = j * UB + i
                    if n + H_AHEAD < UNITS:
                        hidden(n + H_AHEAD)
                    if n + WB_AHEAD < UNITS and (n + WB_AHEAD) % C == 0:
                        weights(n + WB_AHEAD)
                    if i == 0 and j:
                        bias_term(j)
                    output(n)
                    if j == 0 and i == 1:
                        z_transpose(1)
                    if j == 0 and i == 2:
                        logits(1)
                    if i == Y_TR and j:
                        final_transpose(j - 1)
                    if due(R_TR, j, i):
                        r_transpose(due(R_TR, j, i))
                    if due(Z_TR, j, i):
                        z_transpose(due(Z_TR, j, i))
                    if i == W_TR and j + 1 < NB:
                        w_transpose(j + 1)
                    if due(LOGITS, j, i):
                        logits(due(LOGITS, j, i))
            final_transpose(NB - 1)
            final_transpose(NB)

        @block.scalar
        def _(act):
            def copy(dst, src, s, **kw):
                act.activation(dst, src, ACT.Identity, **kw).then_inc(s, 1)

            def sigmoid(b, product, source, into, bias, s):
                act.wait_ge(product, b + 1)
                act.activation(cut(into, b), source[:], ACT.Sigmoid, bias=bias).then_inc(s, 1)

            def transposed(kind, b, into):
                n = turn(kind, b)
                act.wait_ge(tr_mm, n + 1)
                act.activation(into, bank3(7), ACT.Identity).then_inc(tr_out, 1)

            def xnT_out(b):
                transposed("x", b, cut(xnT, b).rearrange("p (t d) -> p t d", d=P))

            def kT_out(b):
                act.wait_ge(k_mm, b + 1)
                copy(cut(kT, b), bank[1][:], kT_ready, bias=col(BK))

            def sig1_out(b):
                sigmoid(b, z1_mm, bank[3], sig1, col(B1), sig1_ready)

            def vT_out(b):
                act.wait_ge(v_mm, b + 1)
                copy(cut(vT, b), bank[2][:], vT_ready, bias=col(BV))

            def qT_out(b):
                act.wait_ge(q_mm, b + 1)
                copy(cut(qT, b), bank[1][:], qT_ready, bias=col(BQ))

            def alr_out(b):
                sigmoid(b, alr_mm, bank[2], alrT, blr_b, alr_ready)

            act.wait_ge(half_ready, 1)
            act.activation(gb_tmp[:, 0:1], minus_half[:, 0:1], ACT.Sigmoid).then_inc(table_ready, 1)
            xnT_out(0)
            act.wait_ge(early_in, 16)
            kT_out(0)
            xnT_out(1)
            vT_out(0)
            sig1_out(0)
            kT_out(1)
            alr_out(0)
            xnT_out(2)
            for w in range(NB + 1):
                if w:
                    transposed("dz2", w - 1, tok(dz2_tok, w - 1))
                if w < NB:
                    sigmoid(w, z2_mm, bank[5], sig2, col(B2), sig2_ready)
                if w + 1 < NB:
                    vT_out(w + 1)
                if w < NB:
                    transposed("k", w, tok(k_tok, w))
                if w == NB:
                    qT_out(1)
                if w + 1 < NB:
                    sig1_out(w + 1)
                if w < NB:
                    transposed("h1", w, tok(h1_tok, w))
                if w + 1 < NB:
                    alr_out(w + 1)
                if w:
                    transposed("dz1", w - 1, tok(dz1_tok, w - 1))
                if w + 2 < NB:
                    kT_out(w + 2)
                if w + 3 < NB:
                    xnT_out(w + 3)
                if w >= NB - 1:
                    qT_out(0 if w < NB else 2)
            qT_out(NB - 1)

            def rsig1_out(b):
                if b == 0:
                    act.wait_ge(bn_ready, 1)
                    act.wait_ge(dz1_done, NB)
                sigmoid(b, rz1_mm, bank[RZ1[b]], r_sig1, bn[:, 0:1], rsig1_ready)

            def rsig2_out(b):
                sigmoid(b, rz2_mm, bank[RZ2[b]], r_sig2, bn[:, 1:2], rsig2_ready)

            def zT_out(b):
                act.wait_ge(zt_tr, b + 1)
                copy(cut(zT, b), bank[7][:], zT_ready, scale=col(G), bias=col(BB))
                copy(cut(z_hi, b), bank[7][:], zhi_done, scale=col(G), bias=col(BB))

            def exponentials(b):
                act.wait_ge(lg_shift, b + 1)
                act.activation(tok(ex, b), tok(lg, b), ACT.Exp).then_inc(ex_ready, 1)

            def wT_out(b):
                act.wait_ge(w_tr, b + 1)
                copy(cut(wT, b), bank[5][:], wT_ready)

            rsig1_out(0)
            rsig1_out(1)
            rsig2_out(0)
            rsig1_out(2)
            rsig1_out(3)
            rsig2_out(1)
            rsig2_out(2)
            rsig2_out(3)
            zT_out(0)
            exponentials(0)

            def gelu(n):
                act.wait_ge(h_mm, n + 1)
                if n >= G_RING:
                    act.wait_ge(t_done, n - G_RING + 1)
                act.activation(g_buf[n % G_RING], bank[n % 2][:], ACT.Gelu,
                               bias=col(FB1 + n % UB)).then_inc(g_done, 1)

            def hi(n):
                act.wait_ge(t_done, n + 1)
                if n >= SPLIT_RING:
                    act.wait_ge(y_mm, n - SPLIT_RING + 1)
                copy(hi_buf[n % SPLIT_RING][:], t_buf[n % T_RING], hi_done)

            for n in range(6):
                gelu(n)
            wT_out(0)
            gelu(6)
            gelu(7)
            hi(0)
            hi(1)
            gelu(8)
            hi(2)
            gelu(9)
            hi(3)
            for j in range(NB):
                for i in range(UB):
                    n = j * UB + i
                    if n + H_AHEAD < UNITS:
                        gelu(n + H_AHEAD)
                    if n + HI_AHEAD < UNITS:
                        hi(n + HI_AHEAD)
                    if j == 0 and i == 1:
                        zT_out(1)
                    if j + 1 < NB and i == EXP[j]:
                        exponentials(j + 1)
                    if due(Z_TR, j, i):
                        zT_out(due(Z_TR, j, i))
                    if i == W_TR and j + 1 < NB:
                        wT_out(j + 1)
                act.wait_ge(y_mm, (j + 1) * UB)
                for q in ([j] if j + 1 < NB else [j, j + 1]):
                    first, count = PARTS[q]
                    act.activation(oT[:, first * P:(first + count) * P],
                                   bank[6][:, (first % TB) * P:(first % TB + count) * P],
                                   ACT.Identity).then_inc(oT_ready, 1)

        @block.vector
        def _(dve):
            steps = [0]

            def step(ins):
                ins.then_inc(dve_step, 1)
                steps[0] += 1
                return steps[0]

            def link(ins):
                count = step(ins)
                yield
                dve.wait_ge(dve_step, count)

            def run(*pieces):
                pieces = list(pieces)
                while pieces:
                    pieces = [p for p in pieces if next(p, "end") != "end"]

            def advance(pieces, count):
                for _ in range(count):
                    next(pieces, None)

            def span(b):
                return slice(TB * b, TB * b + TB)

            def statistics(ln, where, source):
                for i, t in enumerate(where):
                    last = dve.bn_stats(stats[:, t, :], source(i, t))
                yield from link(last)
                for t in where:
                    last = dve.bn_aggr(mv[:, ln, t, :], stats[:, t, :])
                yield from link(last)

            def plus_eps(ln, where):
                dve.tensor_scalar(vpe[:, ln, where], mv[:, ln, where, 1], LN_EPS, None,
                                  ALU.add).then_inc(vpe_ready[ln], 1)

            def normalise(ln, b, into, source, scale):
                for t in tiles(b):
                    last = dve.tensor_scalar(into[:, t, :], source[:, t, :], mv[:, ln, t, 0:1],
                                             scale[:, t:t + 1], ALU.subtract, ALU.mult)
                return last

            def x_stats(b):
                dve.wait_ge(x_in[b], 16)
                run(statistics(LX, tiles(b), lambda i, t: x_tok[:, t, :]))
                plus_eps(LX, span(b))

            def x_norm(b):
                dve.wait_ge(rstd_ready[LX], b + 1)
                normalise(LX, b, xn_tok, x_tok, rstd[:, LX, :]).then_inc(xn_ready, 1)

            def layer1(b):
                dve.wait_ge(sig1_ready, b + 1)
                dve.scalar_tensor_tensor(out=cut(s1, b), in0=bank[3][:], scalar=col(B1),
                                         in1=cut(sig1, b), op0=ALU.add, op1=ALU.mult).then_inc(s1_done, 1)
                dve.wait_ge(s1_done, b + 1)
                dve.tensor_tensor(cut(h1T, b), cut(s1, b), cut(kT, b), ALU.add).then_inc(h1_done, 1)

            def layer1_slope(b):
                dve.scalar_tensor_tensor(out=cut(u1T, b), in0=cut(s1, b), scalar=1.0, in1=cut(sig1, b),
                                         op0=ALU.subtract, op1=ALU.mult).then_inc(u1_done, 1)

            def layer2(b):
                dve.wait_ge(sig2_ready, b + 1)
                dve.scalar_tensor_tensor(out=cut(s2, b), in0=bank[5][:], scalar=col(B2),
                                         in1=cut(sig2, b), op0=ALU.add, op1=ALU.mult).then_inc(s2_done, 1)
                dve.wait_ge(s2_done, b + 1)
                dve.scalar_tensor_tensor(out=cut(u2T, b), in0=cut(s2, b), scalar=1.0, in1=cut(sig2, b),
                                         op0=ALU.subtract, op1=ALU.mult).then_inc(u2_done, 1)
                dve.wait_ge(hv_done, b + 1)
                dve.tensor_tensor(cut(hvT, b), cut(s2, b), cut(hvT, b), ALU.add).then_inc(e_done, 1)
                dve.wait_ge(e_done, b + 1)
                dve.wait_ge(alr_ready, b + 1)
                dve.scalar_tensor_tensor(out=cut(dpT, b), in0=cut(hvT, b), scalar=GRAD_SCALE,
                                         in1=cut(alrT, b), op0=ALU.mult, op1=ALU.mult).then_inc(dp_done, 1)
                dve.wait_ge(dp_done, b + 1)
                dve.wait_ge(d2_done, b + 1)
                dve.scalar_tensor_tensor(out=cut(dz2T, b), in0=cut(dpT, b), scalar=1.0, in1=cut(d2T, b),
                                         op0=ALU.mult, op1=ALU.mult,
                                         accum_out=gb[:, 1, b:b + 1]).then_inc(dz2_done, 1)

            def layer1_back(b):
                dve.wait_ge(dh1_mm, b + 1)
                dve.tensor_tensor(cut(dh1T, b), bank[6][:], cut(dpT, b), ALU.add).then_inc(dh1_done, 1)
                dve.wait_ge(dh1_done, b + 1)
                dve.wait_ge(d1_done, b + 1)
                dve.scalar_tensor_tensor(out=cut(dz1T, b), in0=cut(dh1T, b), scalar=1.0, in1=cut(d1T, b),
                                         op0=ALU.mult, op1=ALU.mult,
                                         accum_out=gb[:, 0, b:b + 1]).then_inc(dz1_done, 1)

            def adam(new, old, g, tmp, rcp, ready):
                yield from link(dve.tensor_scalar(tmp, g, -1.0, ADAM_EPS, ALU.mult, ALU.add))
                yield from link(dve.scalar_tensor_tensor(out=tmp, in0=g, scalar=ADAM_EPS, in1=tmp, op0=ALU.add,
                                              op1=ALU.max))
                yield from link(dve.reciprocal(rcp, tmp))
                yield from link(dve.scalar_tensor_tensor(out=tmp, in0=g, scalar=-LR, in1=rcp, op0=ALU.mult, op1=ALU.mult))
                last = dve.scalar_tensor_tensor(out=new, in0=old, scalar=1.0 - LR * WD, in1=tmp,
                                                op0=ALU.mult, op1=ALU.add)
                last.then_inc(ready, 1)

            x_stats(0)
            x_stats(1)
            x_norm(0)
            x_stats(2)
            x_norm(1)
            x_stats(3)
            x_norm(2)
            dve.wait_ge(early_in, 16)
            x_norm(3)
            for w in range(NB + 1):
                if w < NB:
                    layer1(w)
                if w:
                    layer1_back(w - 1)
                if w < NB:
                    layer1_slope(w)
                    layer2(w)
            dve.wait_ge(late_in, 16)
            dve.wait_ge(gw2_mm, 1)
            run(adam(w2n[:], w2_sb, bank[0][:, 0:P], adam_tmp[:, 0, :], adam_tmp[:, 1, :], w2n_ready))
            dve.wait_ge(dz1_done, NB)
            run(link(dve.tensor_reduce(gbs[:], gb[:], AX_X, ALU.add)))
            dve.wait_ge(w2n_ready, 1)
            dve.wait_ge(gw1_mm, 1)
            run(adam(w1n[:], w1_sb, bank[4][:, 0:P], adam_tmp[:, 0, :], adam_tmp[:, 1, :], w1n_ready),
                adam(bn[:], cols[:, B1:B1 + 2], gbs[:], gb_tmp[:], gb[:, 0, 0:2], bn_ready))
            dve.wait_ge(bn_ready, 1)

            def retrieve1(b):
                dve.wait_ge(rsig1_ready, b + 1)
                dve.scalar_tensor_tensor(out=cut(r_sig1, b), in0=bank[RZ1[b]][:], scalar=bn[:, 0:1],
                                         in1=cut(r_sig1, b), op0=ALU.add, op1=ALU.mult).then_inc(rs1_done, 1)
                dve.wait_ge(rs1_done, b + 1)
                dve.wait_ge(qT_ready, b + 1)
                dve.tensor_tensor(cut(r_h1T, b), cut(r_sig1, b), cut(qT, b), ALU.add).then_inc(rh1_done, 1)

            def retrieve2(b):
                dve.wait_ge(rsig2_ready, b + 1)
                dve.scalar_tensor_tensor(out=cut(r_sig2, b), in0=bank[RZ2[b]][:], scalar=bn[:, 1:2],
                                         in1=cut(r_sig2, b), op0=ALU.add, op1=ALU.mult).then_inc(rs2_done, 1)
                dve.wait_ge(rs2_done, b + 1)
                dve.tensor_tensor(cut(rT, b), cut(r_sig2, b), cut(r_h1T, b), ALU.add).then_inc(r_done, 1)

            def norm_r(b):
                dve.wait_ge(r_tr, b + 1)
                yield from statistics(LR_, tiles(b), lambda i, t: bank[4][:, i * P:(i + 1) * P])
                plus_eps(LR_, span(b))

            def residual(b):
                dve.wait_ge(rstd_ready[LR_], b + 1)
                for i, t in enumerate(tiles(b)):
                    last = dve.scalar_tensor_tensor(out=x1_tok[:, t, :], in0=bank[4][:, i * P:(i + 1) * P],
                                                    scalar=rstd[:, LR_, t:t + 1], in1=x_tok[:, t, :],
                                                    op0=ALU.mult, op1=ALU.add)
                last.then_inc(x1_ready, 1)
                dve.tensor_tensor(shift[:, 0, span(b)], mv[:, LR_, span(b), 0], rstd[:, LR_, span(b)],
                                  ALU.mult).then_inc(shift_ready, 1)
                yield
                dve.wait_ge(x1_ready, b + 1)
                yield from statistics(L1, tiles(b), lambda i, t: x1_tok[:, t, :])
                dve.tensor_scalar(vpe[:, LZ, span(b)], mv[:, L1, span(b), 1], 1.0 + LN_EPS, LN_EPS * LN_EPS,
                                  ALU.mult, ALU.add).then_inc(vpe_ready[LZ], 1)
                plus_eps(L1, span(b))

            def norm_z(b):
                dve.wait_ge(rstd_ready[LZ], b + 1)
                normalise(L1, b, zt_tok, x1_tok, rstd[:, LZ, :]).then_inc(zt_ready, 1)

            def z_low(b):
                dve.wait_ge(zhi_done, b + 1)
                dve.tensor_tensor(cut(z_lo, b), cut(zT, b), cut(z_hi, b).bitcast(F32),
                                  ALU.subtract).then_inc(zlo_done, 1)

            def wide(v):
                return v.unsqueeze(2).to_broadcast([P, TB, E])

            def small(i, b):
                return red[:, i, span(b)]

            MX, SM, RS, M1, F1, M2, F2, DN = range(8)

            def shift_logits(b):
                if b == 0:
                    dve.wait_ge(ramp_ready, 1)
                dve.wait_ge(lg_mm, b + 1)
                dve.tensor_tensor(tok(lg, b), bank[4][:, 0:TB * E].rearrange("p (t e) -> p t e", e=E),
                                  rb_b.unsqueeze(1).to_broadcast([P, TB, E]), ALU.add).then_inc(lg_read, 1)
                yield
                dve.wait_ge(lg_read, b + 1)
                yield from link(dve.tensor_reduce(small(MX, b), tok(lg, b), AX_X, ALU.max))
                dve.tensor_tensor(tok(lg, b), tok(lg, b), wide(small(MX, b)),
                                  ALU.subtract).then_inc(lg_shift, 1)

            def route(b):
                e, p, q, first, second = (tok(v, b) for v in (ex, pr, eq, oh1, oh2))
                total, inverse, top, rank, top2, denom = (small(v, b) for v in (SM, RS, M1, F1, M2, DN))
                done = {}

                def chain(ins):
                    done["chain"] = step(ins)

                def side(make, *operands, **kw):
                    if "side" in done:
                        dve.wait_ge(dve_step, done["side"])
                    done["side"] = step(make(*operands, **kw))

                def chained():
                    yield
                    dve.wait_ge(dve_step, done["chain"])

                dve.wait_ge(ex_ready, b + 1)
                chain(dve.tensor_reduce(top, e, AX_X, ALU.max))
                side(dve.tensor_reduce, total, e, AX_X, ALU.add)
                yield from chained()
                chain(dve.tensor_tensor(q, e, wide(top), ALU.is_equal))
                side(dve.reciprocal, inverse, total)
                yield from chained()
                chain(dve.tensor_tensor(q, q, ramp[:], ALU.mult))
                side(dve.tensor_tensor, p, e, wide(inverse), ALU.mult)
                yield from chained()
                chain(dve.tensor_reduce(rank, q, AX_X, ALU.max))
                yield from chained()
                chain(dve.tensor_tensor(first, q, wide(rank), ALU.is_equal))
                yield from chained()
                chain(dve.scalar_tensor_tensor(out=e, in0=first, scalar=-2.0, in1=e, op0=ALU.mult,
                                               op1=ALU.add))
                yield from chained()
                chain(dve.tensor_reduce(top2, e, AX_X, ALU.max))
                yield from chained()
                chain(dve.tensor_tensor(q, e, wide(top2), ALU.is_equal))
                side(dve.tensor_tensor, denom, top, top2, ALU.add)
                yield from chained()
                chain(dve.tensor_tensor(q, q, ramp[:], ALU.mult))
                side(dve.tensor_tensor, denom, denom, inverse, ALU.mult)
                yield from chained()
                chain(dve.tensor_reduce(rank, q, AX_X, ALU.max))
                side(dve.tensor_scalar, denom, denom, 1e-8, None, ALU.max)
                yield from chained()
                chain(dve.tensor_tensor(second, q, wide(rank), ALU.is_equal))
                side(dve.reciprocal, denom, denom)
                yield from chained()
                chain(dve.tensor_tensor(first, first, second, ALU.add))
                side(dve.tensor_tensor, p, p, wide(denom), ALU.mult)
                yield
                dve.wait_ge(dve_step, done["side"])
                yield from link(dve.tensor_tensor(p, p, first, ALU.mult))
                yield from link(dve.tensor_copy(tok(w_hi, b), p))
                dve.wait_ge(wpad_zero, b + 1)
                dve.tensor_copy(w_pad[:, TB * b:TB * b + TB, 0:E], tok(w_hi, b).bitcast(F32))
                dve.tensor_copy(w_pad[:, TB * b:TB * b + TB, THIRD:THIRD + E], tok(w_hi, b).bitcast(F32))
                dve.tensor_tensor(w_pad[:, TB * b:TB * b + TB, E:2 * E], p,
                                  tok(w_hi, b).bitcast(F32), ALU.subtract).then_inc(w_ready, 1)

            def weigh(n):
                dve.wait_ge(g_done, n + 1)
                if n % C == 0:
                    dve.wait_ge(wb_mm, n // C + 1)
                if n >= T_RING:
                    dve.wait_ge(lo_done, n - T_RING + 1)
                dve.tensor_tensor(t_buf[n % T_RING], g_buf[n % G_RING], bank[2 + n // C % 2][:],
                                  ALU.mult).then_inc(t_done, 1)

            def lo(n):
                dve.wait_ge(hi_done, n + 1)
                dve.tensor_tensor(lo_buf[n % SPLIT_RING][:], t_buf[n % T_RING],
                                  hi_buf[n % SPLIT_RING][:].bitcast(F32), ALU.subtract).then_inc(lo_dve_done, 1)

            def y_stats(q):
                first, count = PARTS[q]
                where = range(first, first + count)
                dve.wait_ge(o_tr, q + 1)
                dve.wait_ge(rstd_ready[L1], first // TB + 1)
                for i, t in enumerate(where):
                    last = dve.scalar_tensor_tensor(out=y_tok[:, t, :], in0=x1_tok[:, t, :],
                                                    scalar=rstd[:, L1, t:t + 1],
                                                    in1=bank[O_BANK[q]][:, i * P:(i + 1) * P],
                                                    op0=ALU.mult, op1=ALU.add)
                last.then_inc(y_ready, 1)
                yield
                dve.wait_ge(y_ready, q + 1)
                yield from statistics(LY, where, lambda i, t: y_tok[:, t, :])
                plus_eps(LY, part_tiles(q))

            def y_norm(q):
                where = part_tiles(q)
                dve.wait_ge(rstd_ready[LY], q + 1)
                dve.wait_ge(shift_ready, where.start // TB + 1)
                yield from link(dve.scalar_tensor_tensor(out=shift[:, 1, where], in0=mv[:, LY, where, 0],
                                                         scalar=-1.0, in1=rstd[:, LY, where],
                                                         op0=ALU.mult, op1=ALU.mult))
                yield from link(dve.tensor_tensor(shift[:, 1, where], shift[:, 1, where],
                                                  shift[:, 0, where], ALU.subtract))
                for t in range(where.start, where.stop):
                    last = dve.tensor_scalar(y_tok[:, t, :], y_tok[:, t, :], rstd[:, LY, t:t + 1],
                                             shift[:, 1, t:t + 1], ALU.mult, ALU.add)
                yield from link(last)
                dve.tensor_tensor(x1_tok[:, where, :], x1_tok[:, where, :], y_tok[:, where, :],
                                  ALU.add).then_inc(yn_done, 1)

            retrieve1(0)
            retrieve1(1)
            retrieve2(0)
            retrieve1(2)
            run(norm_r(0))
            run(residual(0))
            retrieve1(3)
            norm_z(0)
            retrieve2(1)
            retrieve2(2)
            z_low(0)
            run(shift_logits(0))
            retrieve2(3)
            run(route(0))
            dve.wait_ge(b2hi_done, 1)
            low = slice(THIRD, 2 * THIRD)
            dve.tensor_tensor(b2_parts[low, :], b2_stack[low, :], b2_parts[low, :].bitcast(F32),
                              ALU.subtract).then_inc(b2lo_done, 1)
            run(norm_r(1))
            x1 = residual(1)
            weigh(0)
            weigh(1)
            advance(x1, 1)
            weigh(2)
            advance(x1, 1)
            weigh(3)
            run(x1)
            r_stats = iter(())
            for j in range(NB):
                result_stats, result = y_stats(j - 1), y_norm(j - 1)
                logits_shift, routing = shift_logits(j + 1), route(j + 1)
                for i in range(UB):
                    n = j * UB + i
                    if n + T_AHEAD < UNITS:
                        weigh(n + T_AHEAD)
                    if n + LO_AHEAD in LO_ON_DVE:
                        lo(n + LO_AHEAD)
                    if j:
                        if i >= Y_STATS:
                            advance(result_stats, 1)
                        if i >= Y_NORM:
                            advance(result, 2)
                    if j == 0 and i == 0:
                        norm_z(1)
                    if j == 0 and i == 2:
                        z_low(1)
                    if j + 1 < NB:
                        if i == ROUTER[j]:
                            run(logits_shift)
                        if i >= ROUTE[j]:
                            advance(routing, ROUTE_STEPS[j])
                        if i == W_TR - 1:
                            run(routing)
                    if due(NORM_R, j, i):
                        r_stats = norm_r(due(NORM_R, j, i))
                    if due(RESIDUAL, j, i):
                        x1 = residual(due(RESIDUAL, j, i))
                    advance(r_stats, 1)
                    advance(x1, 1)
                    if due(NORM_Z, j, i):
                        norm_z(due(NORM_Z, j, i))
                    if due(Z_LOW, j, i):
                        z_low(due(Z_LOW, j, i))
            run(y_stats(NB - 1), y_stats(NB))
            run(y_norm(NB - 1), y_norm(NB))


_OUTS = [((8, 256, 128), 'float32')]


def kernel(**inputs):
    import numpy as _np
    import concourse.bacc as _bacc
    from concourse import mybir as _mybir
    from concourse.bass_utils import run_bass_kernel_spmd as _run

    a = {name[3:]: _np.asarray(value) for name, value in inputs.items()}
    E, D, HF = a["ffn_W1"].shape
    vectors = [a[f"attn_{n}"] for n in ("bk", "bq", "bv", "b1", "b2")] + [a["ffn_ln_g"], a["ffn_ln_b"]]
    parts = {
        "Wk": a["attn_Wk"], "Wv": a["attn_Wv"], "W1": a["attn_W1"],
        "Wlr": _np.broadcast_to(a["attn_Wlr"], (D, D)), "blr": _np.broadcast_to(a["attn_blr"], (D, 1)),
        "vectors": _np.stack(vectors + list(a["ffn_b1"].reshape(-1, D)), axis=1),
        "W2": a["attn_W2"], "W2T": a["attn_W2"].T, "Wq": a["attn_Wq"], "rW": a["ffn_rW"],
        "rb": _np.broadcast_to(a["ffn_rb"], (D, E)),
        "b2": _np.concatenate([a["ffn_b2"], a["ffn_b2"], _np.zeros((32 - 2 * E, D), a["ffn_b2"].dtype),
                               a["ffn_b2"], _np.zeros((D - 32 - E, D), a["ffn_b2"].dtype)]),
    }
    early, late = (_np.concatenate([parts[n] for n in at], axis=1) for at, _ in widths(D, E, HF))

    nc = _bacc.Bacc("TRN2", target_bir_lowering=False, num_devices=1)
    arrays, args = {}, []
    for name, value in (("x", a["attn_x"]), ("early", early), ("late", late), ("fW1", a["ffn_W1"]),
                        ("fW2", a["ffn_W2"])):
        value = _np.ascontiguousarray(value)
        arrays[f"in_{name}_dram"] = value
        args.append(nc.dram_tensor(f"in_{name}_dram", value.shape, _mybir.dt.from_np(value.dtype),
                                   kind="ExternalInput").ap())
    for i, (shape, dtype) in enumerate(_OUTS):
        dt = _mybir.dt.from_np(_np.dtype(dtype))
        args.append(nc.dram_tensor(f"out_{i}_dram", shape, dt, kind="ExternalOutput").ap())
    memory_and_experts(nc, *args)
    r = _run(nc, [arrays], core_ids=[0])
    return r.results[0]["out_0_dram"]
```
